# Optimizing a Trainium2 kernel written in Bass

```python
import numpy as np
import jax
import jax.numpy as jnp

def _softmax(x, axis=-1):
    return jax.nn.softmax(x, axis=axis)

def _gelu(x):
    return jax.nn.gelu(x, approximate=True)

def _silu(x):
    return jax.nn.silu(x)

def _sigmoid(x):
    return jax.nn.sigmoid(x)

def _layernorm(x, axis=-1, eps=1e-05):
    m = jnp.mean(x, axis=axis, keepdims=True)
    v = jnp.var(x, axis=axis, keepdims=True)
    return (x - m) / jnp.sqrt(v + eps)

def _scatter_add(tgt, idx, src, axis=0):
    return tgt.at[idx].add(src)

def _segment_sum(src, seg, n):
    return jax.ops.segment_sum(src, seg, n)
kernel_name = 'mk_gnn_resnorm_d2_gnn_r8_b80844'

def setup_inputs(seed: int=0):
    np.random.seed(seed)
    _w = jnp.asarray

    def _rec_inputs():
        import jax
        import jax.numpy as jnp
        _gk = jax.random.key(seed)
        x = 1.875e-05 + 1 * jax.random.normal(jax.random.fold_in(_gk, 1), (6250, 96), jnp.float32)
        _s = jax.random.randint(jax.random.fold_in(_gk, 2), (100000,), 0, 6250, jnp.int32)
        _d = jax.random.randint(jax.random.fold_in(_gk, 3), (100000,), 0, 6250, jnp.int32)
        _loop = jnp.arange(6250, dtype=jnp.int32)
        src = jnp.concatenate([_s, _d, _loop])
        dst = jnp.concatenate([_d, _s, _loop])
        _o = jnp.argsort(dst, stable=True)
        src = src[_o]
        dst = dst[_o]
        edge_attr_96 = 5.93493e-05 + 1.00006 * jax.random.normal(jax.random.fold_in(_gk, 11), (206250, 96), jnp.float32)
        return (x, src, dst, edge_attr_96)
    x, src, dst, edge_attr_96 = _rec_inputs()

    def _L0_gnn_setup():
        import jax, jax.numpy as jnp
        import numpy as np
        N_NODES = 12500
        N_EDGES = 100000
        D = 96
        BN_EPS = 1e-05
        LEAKY_SLOPE = 0.01

        def _batch_norm(h, gamma, beta):
            mu = h.mean(axis=0)
            var = jnp.mean(jnp.square(h - mu), axis=0)
            return gamma * (h - mu) * jax.lax.rsqrt(var + BN_EPS) + beta

        def _forward(x, edge_index, W_self1, W_neigh1, W_pool, b_pool, W_self2, W_neigh2, g1, beta1, g2, beta2):
            src, dst = (edge_index[0], edge_index[1])
            n = x.shape[0]
            deg = jax.ops.segment_sum(jnp.ones((src.shape[0],), x.dtype), dst, num_segments=n)
            agg_sum = jax.ops.segment_sum(x[src], dst, num_segments=n)
            h_mean = agg_sum / jnp.maximum(deg, 1.0)[:, None]
            out1 = x @ W_self1 + h_mean @ W_neigh1
            out1 = _batch_norm(out1, g1, beta1)
            hp = jax.nn.relu(x @ W_pool + b_pool)
            agg_max = jax.ops.segment_max(hp[src], dst, num_segments=n)
            h_max = jnp.where(deg[:, None] > 0, agg_max, 0.0)
            out2 = x @ W_self2 + h_max @ W_neigh2
            out2 = _batch_norm(out2, g2, beta2)
            return jax.nn.leaky_relu(out1 + out2, negative_slope=LEAKY_SLOPE)
        key = jax.random.key(seed)
        ks = jax.random.split(key, 9)
        x = jax.random.normal(ks[0], (N_NODES, D), dtype=jnp.float32)
        edge_index = jax.random.randint(ks[1], (2, N_EDGES), 0, N_NODES, dtype=jnp.int64)
        s = 0.05
        return {'x': x, 'edge_index': edge_index, 'W_self1': jax.random.normal(ks[2], (D, D), dtype=jnp.float32) * s, 'W_neigh1': jax.random.normal(ks[3], (D, D), dtype=jnp.float32) * s, 'W_pool': jax.random.normal(ks[4], (D, D), dtype=jnp.float32) * s, 'b_pool': jax.random.normal(ks[5], (D,), dtype=jnp.float32) * s, 'W_self2': jax.random.normal(ks[6], (D, D), dtype=jnp.float32) * s, 'W_neigh2': jax.random.normal(ks[7], (D, D), dtype=jnp.float32) * s, 'g1': jnp.ones((D,), jnp.float32), 'beta1': jnp.zeros((D,), jnp.float32), 'g2': jnp.ones((D,), jnp.float32), 'beta2': jnp.zeros((D,), jnp.float32)}
    _L0_gnn_all = _L0_gnn_setup()
    _L0_gnn_in = {k: v for k, v in _L0_gnn_all.items() if k in ('W_self1', 'W_neigh1', 'W_pool', 'b_pool', 'W_self2', 'W_neigh2', 'g1', 'beta1', 'g2', 'beta2')}
    del _L0_gnn_all

    def _L1_gnn_setup():
        import jax, jax.numpy as jnp
        import numpy as np
        N_NODES = 6250
        N_EDGES = 100000
        IN_DIM = 96
        NUM_HEADS = 8
        HEAD_DIM = IN_DIM // NUM_HEADS
        key = jax.random.key(seed)
        ks = jax.random.split(key, 11)
        s = 1.0 / np.sqrt(IN_DIM)
        return {'x': jax.random.normal(ks[0], (N_NODES, IN_DIM), dtype=jnp.float32), 'edge_index': jax.random.randint(ks[1], (2, N_EDGES), 0, N_NODES, dtype=jnp.int64), 'edge_attr': jax.random.normal(ks[2], (N_EDGES, IN_DIM), dtype=jnp.float32), 'Wq': jax.random.normal(ks[3], (IN_DIM, IN_DIM), dtype=jnp.float32) * s, 'bq': jax.random.normal(ks[4], (IN_DIM,), dtype=jnp.float32) * s, 'Wk': jax.random.normal(ks[5], (IN_DIM, IN_DIM), dtype=jnp.float32) * s, 'bk': jax.random.normal(ks[6], (IN_DIM,), dtype=jnp.float32) * s, 'We': jax.random.normal(ks[7], (IN_DIM, IN_DIM), dtype=jnp.float32) * s, 'be': jax.random.normal(ks[8], (IN_DIM,), dtype=jnp.float32) * s, 'Wv': jax.random.normal(ks[9], (IN_DIM, IN_DIM), dtype=jnp.float32) * s, 'bv': jax.random.normal(ks[10], (IN_DIM,), dtype=jnp.float32) * s}
    _L1_gnn_all = _L1_gnn_setup()
    _L1_gnn_in = {k: v for k, v in _L1_gnn_all.items() if k in ('Wq', 'bq', 'Wk', 'bk', 'We', 'be', 'Wv', 'bv')}
    del _L1_gnn_all
    return {'x': x, 'src': src, 'dst': dst, 'edge_attr_96': edge_attr_96, 'L0_gnn_W_self1': _L0_gnn_in['W_self1'], 'L0_gnn_W_neigh1': _L0_gnn_in['W_neigh1'], 'L0_gnn_W_pool': _L0_gnn_in['W_pool'], 'L0_gnn_b_pool': _L0_gnn_in['b_pool'], 'L0_gnn_W_self2': _L0_gnn_in['W_self2'], 'L0_gnn_W_neigh2': _L0_gnn_in['W_neigh2'], 'L0_gnn_g1': _L0_gnn_in['g1'], 'L0_gnn_beta1': _L0_gnn_in['beta1'], 'L0_gnn_g2': _L0_gnn_in['g2'], 'L0_gnn_beta2': _L0_gnn_in['beta2'], 'L1_gnn_Wq': _L1_gnn_in['Wq'], 'L1_gnn_bq': _L1_gnn_in['bq'], 'L1_gnn_Wk': _L1_gnn_in['Wk'], 'L1_gnn_bk': _L1_gnn_in['bk'], 'L1_gnn_We': _L1_gnn_in['We'], 'L1_gnn_be': _L1_gnn_in['be'], 'L1_gnn_Wv': _L1_gnn_in['Wv'], 'L1_gnn_bv': _L1_gnn_in['bv']}

def reference(x, src, dst, edge_attr_96, L0_gnn_W_self1, L0_gnn_W_neigh1, L0_gnn_W_pool, L0_gnn_b_pool, L0_gnn_W_self2, L0_gnn_W_neigh2, L0_gnn_g1, L0_gnn_beta1, L0_gnn_g2, L0_gnn_beta2, L1_gnn_Wq, L1_gnn_bq, L1_gnn_Wk, L1_gnn_bk, L1_gnn_We, L1_gnn_be, L1_gnn_Wv, L1_gnn_bv):
    import jax
    import jax.numpy as jnp

    def _L0_gnn_ref(x, edge_index, W_self1, W_neigh1, W_pool, b_pool, W_self2, W_neigh2, g1, beta1, g2, beta2):
        import jax, jax.numpy as jnp
        import numpy as np
        N_NODES = 12500
        N_EDGES = 100000
        D = 96
        BN_EPS = 1e-05
        LEAKY_SLOPE = 0.01

        def _batch_norm(h, gamma, beta):
            mu = h.mean(axis=0)
            var = jnp.mean(jnp.square(h - mu), axis=0)
            return gamma * (h - mu) * jax.lax.rsqrt(var + BN_EPS) + beta

        def _forward(x, edge_index, W_self1, W_neigh1, W_pool, b_pool, W_self2, W_neigh2, g1, beta1, g2, beta2):
            src, dst = (edge_index[0], edge_index[1])
            n = x.shape[0]
            deg = jax.ops.segment_sum(jnp.ones((src.shape[0],), x.dtype), dst, num_segments=n)
            agg_sum = jax.ops.segment_sum(x[src], dst, num_segments=n)
            h_mean = agg_sum / jnp.maximum(deg, 1.0)[:, None]
            out1 = x @ W_self1 + h_mean @ W_neigh1
            out1 = _batch_norm(out1, g1, beta1)
            hp = jax.nn.relu(x @ W_pool + b_pool)
            agg_max = jax.ops.segment_max(hp[src], dst, num_segments=n)
            h_max = jnp.where(deg[:, None] > 0, agg_max, 0.0)
            out2 = x @ W_self2 + h_max @ W_neigh2
            out2 = _batch_norm(out2, g2, beta2)
            return jax.nn.leaky_relu(out1 + out2, negative_slope=LEAKY_SLOPE)
        return _forward(x, edge_index, W_self1, W_neigh1, W_pool, b_pool, W_self2, W_neigh2, g1, beta1, g2, beta2)

    def _L1_gnn_ref(x, edge_index, edge_attr, Wq, bq, Wk, bk, We, be, Wv, bv):
        import jax, jax.numpy as jnp
        import numpy as np
        N_NODES = 6250
        N_EDGES = 100000
        IN_DIM = 96
        NUM_HEADS = 8
        HEAD_DIM = IN_DIM // NUM_HEADS
        N = x.shape[0]
        H, D = (NUM_HEADS, HEAD_DIM)
        Q_h = (x @ Wq + bq).reshape(N, H, D)
        K_h = (x @ Wk + bk).reshape(N, H, D)
        V_h = (x @ Wv + bv).reshape(N, H, D)
        E = (edge_attr @ We + be).reshape(-1, H, D)
        src_idx = edge_index[0]
        dst_idx = edge_index[1]
        src = K_h[src_idx]
        dest = Q_h[dst_idx]
        score = src * dest / jnp.sqrt(jnp.asarray(D, x.dtype))
        score = score * E
        score = jnp.exp(jnp.clip(score.sum(-1, keepdims=True), -5.0, 5.0))
        msg = V_h[src_idx] * score
        wV = jax.ops.segment_sum(msg, dst_idx, num_segments=N)
        Z = jax.ops.segment_sum(score, dst_idx, num_segments=N)
        h_out = wV / (Z + 1e-06)
        return h_out.reshape(N, H * D)
    edge_index = jnp.stack([src, dst])
    x = _layernorm(x + _L0_gnn_ref(x, edge_index, L0_gnn_W_self1, L0_gnn_W_neigh1, L0_gnn_W_pool, L0_gnn_b_pool, L0_gnn_W_self2, L0_gnn_W_neigh2, L0_gnn_g1, L0_gnn_beta1, L0_gnn_g2, L0_gnn_beta2), axis=-1)
    x = _layernorm(x + _L1_gnn_ref(x, edge_index, edge_attr_96, L1_gnn_Wq, L1_gnn_bq, L1_gnn_Wk, L1_gnn_bk, L1_gnn_We, L1_gnn_be, L1_gnn_Wv, L1_gnn_bv), axis=-1)
    return x

_drawn_inputs = setup_inputs


def setup_inputs(seed=0):
    import zlib

    import numpy as np

    out = dict(_drawn_inputs(seed))
    spreads = {'L0_gnn_g1': (1.0, 0.2),
     'L0_gnn_beta1': (0.0, 0.1),
     'L0_gnn_g2': (1.0, 0.2),
     'L0_gnn_beta2': (0.0, 0.1)}
    factors = {'L0_gnn_b_pool': 41.174}
    for name, (base, spread) in spreads.items():
        noise = np.random.default_rng([zlib.crc32(name.encode()), seed]).standard_normal(out[name].shape)
        drawn = base * np.exp(spread * noise) if base else spread * noise
        out[name] = jnp.asarray(drawn.astype(out[name].dtype))
    for name, factor in factors.items():
        out[name] = (out[name] * factor).astype(out[name].dtype)
    return out
```

```python
import concourse.bass as bass
from concourse import mybir
from contextlib import ExitStack

F32 = mybir.dt.float32
BF16 = mybir.dt.bfloat16
I32 = mybir.dt.int32
ALU = mybir.AluOpType
ACT = mybir.ActivationFunctionType
AX = mybir.AxisListType

N, D, E = 6250, 96, 206250
H = 8
HD = D // H
P = 128
J = 4
GE = P * J
FULL = E // GE
TAIL = E - FULL * GE
R = 4
TURNS = -(-(FULL + 1) // R)
NG = TURNS * R
W = 64
NT = -(-N // P)
NFULL = N // P
NTAIL = N - NFULL * P
NP = NT * P
K7 = 7
CH = NP // 14
BNC = 250
XROW = 2 * D + 1
DSUM = D + 1
DMSG = D + H
PAD_DST = 20000
EPS = 1e-5
AHEAD = 4


def build(nc, x, src_m, src_t, dst_m, dst_t, prv_m, prv_t, nxt_m, nxt_t, edge_attr, Ws1, Wn1, Wp, bp, Ws2, Wn2,
          g1, be1, g2, be2, Wq, bq, Wk, bk, We, be, Wv, bv, out):
    ctx = ExitStack()
    with ctx:
        def sb(name, shape, dt=F32):
            return ctx.enter_context(nc.sbuf_tensor(name, shape, dt))

        def sem(name):
            return ctx.enter_context(nc.semaphore(name))

        x_table = nc.dram_tensor("x_table", (NP, XROW), F32, kind="Internal").ap()
        kv_table = nc.dram_tensor("kv_table", (NP, 2 * D), F32, kind="Internal").ap()
        q_table = nc.dram_tensor("q_table", (NP, D), F32, kind="Internal").ap()

        xN = sb("xN", [P, NT, D])
        stage = sb("stage", [P, NT * XROW])
        xT = sb("xT", [DSUM, NP])
        acc = sb("acc", [P, 2, NP])
        qN = acc[:, 1, 0:NT * D].rearrange("p (t c) -> p t c", t=NT)
        dst_i = acc[:, 1, 0:NG * J].bitcast(I32)
        nbr_i = acc[:, 1, NG * J:2 * NG * J].bitcast(I32)
        tmpE = acc[:, 1, 2 * NG * J:3 * NG * J].rearrange("p (g j) -> p g j", j=J)
        x_stage = stage[:, :].rearrange("p (t c) -> p t c", t=NT)
        kv_stage = stage[:, 0:NT * 2 * D].rearrange("p (t c) -> p t c", t=NT)
        h_stage = stage[:, 0:NT * DMSG].rearrange("p (t c) -> p t c", t=NT)

        src_all = sb("src_all", [P, (NG + R) * J], I32)
        rel = sb("rel", [P, NG, 2, J])
        keep = sb("keep", [P, NG, J], BF16)
        baseB = sb("baseB", [P, NG])
        base_i = sb("base_i", [1, NG], I32)
        idx = sb("idx", [P, R, J], I32)

        gat = sb("gat", [P, R, J, XROW])
        kvg = gat[:, :, :, 0:2 * D]
        S = sb("S", [P, 2, 2 * J, W])
        keepC = sb("keepC", [D, 2, GE], BF16)
        scan = sb("scan", [D, 2, GE])
        scanE = sb("scanE", [P, 2, J, DSUM])
        ea = sb("ea", [P, R, J, D])
        qwin = sb("qwin", [W, R, D])
        eaC = sb("eaC", [DSUM, 2, GE])
        stC = scan[0:W, :, :]
        prod = sb("prod", [P, 2, J * D])
        sc = sb("sc", [P, 2, J * H])
        msg = sb("msg", [P, 2, J, DMSG])

        ident = sb("ident", [P, P])
        identb = sb("identb", [P, P], BF16)
        first_row = sb("first_row", [P, P])
        last_row = sb("last_row", [DSUM, D])
        iotaW = sb("iotaW", [P, W])
        w_self1 = sb("w_self1", [D, D])
        w_neigh1 = sb("w_neigh1", [D, D])
        w_self2 = sb("w_self2", [D, D])
        w_neigh2 = sb("w_neigh2", [D, D])
        w_pool = sb("w_pool", [DSUM, D])
        w_kv = sb("w_kv", [DSUM, 2 * D])
        w_q = sb("w_q", [DSUM, D])
        w_e = sb("w_e", [DSUM, D])
        gb = sb("gb", [D, 4])
        eps_col = sb("eps_col", [P, 1])
        meanT = prod[0:D, :, :].rearrange("p b c -> p (b c)")[:, 0:CH]
        stats = sb("stats", [D, 2, N // BNC, 6])
        mv = sb("mv", [D, 2, 2])
        std = sb("std", [D, 2])
        rstd = sb("rstd", [D, 2])
        ga = sb("ga", [D, 2])
        sh = sb("sh", [D, 2])
        shs = sb("shs", [D, 1])
        nmean = sb("nmean", [P, NT])
        nvar = sb("nvar", [P, NT])
        nrz = prod[:, :, :].rearrange("p b c -> p (b c)")[:, 0:NT * H].rearrange("p (t h) -> p t h", t=NT)

        bank = [ctx.enter_context(nc.psum_tensor(f"bank{k}", [P, 512], F32)) for k in range(8)]

        s_x, s_w, s_wb, s_gb = sem("s_x"), sem("s_w"), sem("s_wb"), sem("s_gb")
        s_src, s_dst, s_prv, s_nxt = sem("s_src"), sem("s_dst"), sem("s_prv"), sem("s_nxt")
        s_xtab, s_kvtab, s_out = sem("s_xtab"), sem("s_kvtab"), sem("s_out")
        s_gat = [sem(f"s_gat{r}") for r in range(R)]
        s_kvg = [sem(f"s_kvg{r}") for r in range(R)]
        s_ea = [sem(f"s_ea{r}") for r in range(R)]
        s_qw = [sem(f"s_qw{r}") for r in range(R)]
        s_tail = sem("s_tail")
        s_zero, s_pads, s_iden = sem("s_zero"), sem("s_pads"), sem("s_iden")
        s_v = sem("s_v")
        s_base, s_baseP, s_rel = sem("s_base"), sem("s_baseP"), sem("s_rel")
        s_xT_p, s_xT_c, s_hp_p, s_hp_c = sem("s_xT_p"), sem("s_xT_c"), sem("s_hp_p"), sem("s_hp_c")
        s_xst = sem("s_xst")
        s_idx, s_free0, s_S, s_hpT, s_keepP, s_keepC = (sem("s_idx"), sem("s_free0"), sem("s_S"), sem("s_hpT"),
                                                        sem("s_keepP"), sem("s_keepC"))
        s_sum, s_scan, s_back, s_bcp, s_max, s_acc = (sem("s_sum"), sem("s_scan"), sem("s_back"), sem("s_bcp"),
                                                      sem("s_max"), sem("s_acc"))
        s_deg, s_mean, s_lin, s_linc, s_bn, s_std = (sem("s_deg"), sem("s_mean"), sem("s_lin"), sem("s_linc"),
                                                     sem("s_bn"), sem("s_std"))
        s_hT, s_hN_p, s_hN_c, s_var, s_sd, s_x1 = (sem("s_hT"), sem("s_hN_p"), sem("s_hN_c"), sem("s_var"),
                                                   sem("s_sd"), sem("s_x1"))
        s_x1_p, s_x1_c, s_kv_p, s_kv_c, s_q_c = (sem("s_x1_p"), sem("s_x1_c"), sem("s_kv_p"), sem("s_kv_c"),
                                                 sem("s_q_c"))
        s_idx2, s_S2, s_T, s_tc, s_EQ = sem("s_idx2"), sem("s_S2"), sem("s_T"), sem("s_tc"), sem("s_EQ")
        s_p1, s_p2, s_p3, s_clip, s_exp = sem("s_p1"), sem("s_p2"), sem("s_p3"), sem("s_clip"), sem("s_exp")
        s_msg, s_agg, s_acc2 = sem("s_msg"), sem("s_agg"), sem("s_acc2")
        s_wv_p, s_wv_c, s_fin, s_tick = sem("s_wv_p"), sem("s_wv_c"), sem("s_fin"), sem("s_tick")

        def ready(i, r):
            return i * R + (r + 1 + AHEAD)

        def freed(i, r, depth):
            return i * R + (r + 1 + AHEAD - depth)

        block = ctx.enter_context(nc.Block())

        @block.sync
        def _(sp):
            sp.wait_ge(s_zero, 1)
            sp.dma_start(xN[:, 0:NFULL, :], x[0:NFULL * P, :].rearrange("(t p) c -> p t c", p=P)).then_inc(s_x, 16)
            sp.dma_start(xN[0:NTAIL, NFULL, :], x[NFULL * P:N, :]).then_inc(s_x, 16)
            for w, v in ((w_self1, Ws1), (w_neigh1, Wn1), (w_self2, Ws2), (w_neigh2, Wn2)):
                sp.dma_start(w[:, :], v[:, :]).then_inc(s_w, 16)
            for w, v, b in ((w_pool[:, :], Wp, bp), (w_kv[:, 0:D], Wk, bk), (w_kv[:, D:2 * D], Wv, bv),
                            (w_q[:, :], Wq, bq), (w_e[:, :], We, be)):
                sp.dma_start(w[0:D, :], v[:, :]).then_inc(s_wb, 16)
                sp.dma_start(w[D:D + 1, :], b.rearrange("(a c) -> a c", a=1)).then_inc(s_wb, 16)
            with nc.allow_non_contiguous_dma(reason="four columns of 96 numbers"):
                for n, v in enumerate((g1, be1, g2, be2)):
                    sp.dma_start(gb[:, n:n + 1], v.rearrange("(c a) -> c a", a=1)).then_inc(s_gb, 16)

            def edges(to, main, tail, done):
                n = tail.shape[0]
                sp.dma_start(to[:, 0:FULL * J], main).then_inc(done, 16)
                sp.dma_start(to[0:n // J, FULL * J:(FULL + 1) * J],
                             tail[0:n // J * J].rearrange("(p j) -> p j", j=J)).then_inc(done, 16)
                sp.dma_start(to[n // J:n // J + 1, FULL * J:FULL * J + n % J],
                             tail[n // J * J:n].rearrange("(a j) -> a j", a=1)).then_inc(done, 16)

            sp.wait_ge(s_pads, 3)
            edges(src_all, src_m, src_t, s_src)
            edges(dst_i, dst_m, dst_t, s_dst)
            edges(nbr_i, prv_m, prv_t, s_prv)
            sp.wait_ge(s_pads, 4)
            edges(nbr_i, nxt_m, nxt_t, s_nxt)
            sp.wait_ge(s_xst, 1)
            sp.wait_ge(s_hp_c, NT)
            sp.dma_start(x_table.rearrange("(t p) c -> p t c", p=P), x_stage).then_inc(s_xtab, 16)

            sp.wait_ge(s_kv_c, NT)
            sp.wait_ge(s_q_c, NT)
            sp.dma_start(kv_table.rearrange("(t p) c -> p t c", p=P), kv_stage).then_inc(s_kvtab, 16)
            sp.dma_start(q_table.rearrange("(t p) c -> p t c", p=P), qN[:, :, :]).then_inc(s_kvtab, 16)
            sp.wait_ge(s_kvtab, 32)

            ea_v = edge_attr[0:FULL * GE, :].rearrange("(g p j) c -> p g (j c)", p=P, j=J)

            def load_group(i, r, ea_src):
                sp.wait_ge(s_T, freed(i, r, R))
                if ea_src is not None:
                    ea_src()
                sp.wait_ge(s_EQ, freed(i, r, R))
                base = sp.value_load(base_i[0:1, bass.ds(i * R + r, 1)], min_val=0, max_val=N - W)
                sp.dma_start(qwin[:, r, :], q_table[bass.ds(base, W), :]).then_inc(s_qw[r], 16)

            with sp.Fori(0, FULL // R) as i:
                for r in range(R):
                    load_group(i, r, lambda: sp.dma_start(
                        ea[:, r, :, :].rearrange("p j c -> p (j c)"),
                        ea_v[:, bass.ds(i * R + r, 1), :].rearrange("p g c -> p (g c)")).then_inc(s_ea[r], 16))

            def tail_load(g, r):
                if g < FULL:
                    sp.dma_start(ea[:, r, :, :].rearrange("p j c -> p (j c)"), ea_v[:, g, :]).then_inc(s_ea[r], 16)
                elif g == FULL:
                    e0, whole = FULL * GE, TAIL // J
                    sp.dma_start(ea[0:whole, r, :, :].rearrange("p j c -> p (j c)"),
                                 edge_attr[e0:e0 + whole * J, :].rearrange("(p j) c -> p (j c)", j=J)
                                 ).then_inc(s_tail, 16)
                    sp.wait_ge(s_tail, 16)
                    sp.dma_start(ea[whole:whole + 1, r, 0:TAIL % J, :].rearrange("p j c -> p (j c)"),
                                 edge_attr[e0 + whole * J:E, :].rearrange("(a j) c -> a (j c)", a=1)
                                 ).then_inc(s_ea[r], 16)
                else:
                    sp.sem_inc(s_ea[r], 16)

            for g in range(FULL // R * R, NG):
                load_group(g // R, g % R, lambda: tail_load(g, g % R))

            sp.wait_ge(s_fin, 1)
            sp.dma_start(out[0:NFULL * P, :].rearrange("(t p) c -> p t c", p=P), xN[:, 0:NFULL, :]).then_inc(s_out, 16)
            sp.dma_start(out[NFULL * P:N, :], xN[0:NTAIL, NFULL, :]).then_inc(s_out, 16)
            sp.wait_ge(s_out, 32)

        @block.gpsimd
        def _(pool):
            pool.memset(xN[:, NFULL, :], 0.0).then_inc(s_zero, 1)
            pool.memset(ident[:, :], 0.0).then_inc(s_iden, 1)
            pool.memset(first_row[:, :], 1.0).then_inc(s_iden, 1)
            pool.iota(iotaW[:, :], pattern=[[1, W]], base=0, channel_multiplier=0,
                      allow_small_or_imprecise_dtypes=True).then_inc(s_iden, 1)
            pool.wait_ge(s_iden, 3)
            pool.affine_select(out=ident[:, :], in_=ident[:, :], compare_op=ALU.not_equal, fill=1.0, base=0,
                               pattern=[[-1, P]], channel_multiplier=1).then_inc(s_iden, 1)
            pool.affine_select(out=first_row[:, :], in_=first_row[:, :], compare_op=ALU.is_equal, fill=0.0, base=0,
                               pattern=[[0, P]], channel_multiplier=1).then_inc(s_iden, 1)
            pool.wait_ge(s_iden, 5)
            pool.tensor_copy(identb[:, :], ident[:, :]).then_inc(s_iden, 1)

            def gathers(table, width, s_i, s_free, s_done, turn_of):
                with pool.Fori(0, TURNS) as i:
                    for r in range(R):
                        pool.wait_ge(s_i, ready(i, r))
                        pool.sem_inc(s_tick, 1)
                        pool.wait_ge(s_free, freed(i, r, R))
                        pool.sem_inc(s_tick, 1)
                        for j in range(J):
                            pool.indirect_dma_start(
                                out=gat[:, r, j, 0:width], out_offset=None, in_=table,
                                in_offset=bass.IndirectOffsetOnAxis(ap=idx[:, r, j:j + 1], axis=0)
                            ).then_inc(s_done[r], 16)

            pool.wait_ge(s_xtab, 16)
            gathers(x_table, XROW, s_idx, s_sum, s_gat, None)
            pool.wait_ge(s_kvtab, 32)
            gathers(kv_table, 2 * D, s_idx2, s_msg, s_kvg, None)

        def copy_indices(act, i, r, s_done, s_i):
            act.wait_ge(s_done[r], i * (16 * J) + 16 * J)
            act.copy(idx[:, r, :], src_all[:, bass.ds((i * R + (r + R)) * J, J)]).then_inc(s_i, 1)

        @block.scalar
        def _(act):
            for s in (s_keepC, s_bcp, s_tc, s_exp):
                act.sem_inc(s, AHEAD)
            with act.Fori(0, NT // K7) as i:
                for k in range(K7):
                    act.wait_ge(s_xT_p, i * K7 + (k + 1))
                    act.copy(xT[0:D, bass.ds((i * K7 + k) * P, P)], bank[k][0:D, 0:P]).then_inc(s_xT_c, 1)
            act.wait_ge(s_src, 48)
            act.copy(idx[:, :, :].rearrange("p r j -> p (r j)"), src_all[:, 0:R * J]).then_inc(s_idx, R + AHEAD)

            with act.Fori(0, TURNS) as i:
                def keep_copy(r):
                    copy_indices(act, i, r, s_gat, s_idx)
                    act.wait_ge(s_keepP, ready(i, r))
                    act.wait_ge(s_scan, freed(i, r, 2))
                    act.copy(keepC[:, r % 2, :], bank[2 + r % 2][0:D, :]).then_inc(s_keepC, 1)

                def back_copy(r):
                    act.wait_ge(s_back, ready(i, r))
                    act.wait_ge(s_max, freed(i, r, 2))
                    act.copy(scanE[:, r % 2, :, 0:D],
                             bank[4 + r % 2][:, 0:J * D].rearrange("p (j c) -> p j c", j=J)).then_inc(s_bcp, 1)

                keep_copy(0)
                keep_copy(1)
                back_copy(0)
                keep_copy(2)
                back_copy(1)
                keep_copy(3)
                back_copy(2)
                back_copy(3)

            with act.Fori(0, NP // CH) as i:
                act.wait_ge(s_lin, i + 1)
                for m in range(2):
                    last = act.copy(acc[0:D, m, bass.ds(i * CH, CH)], bank[1 + m][0:D, 0:CH])
                last.then_inc(s_linc, 1)
            act.wait_ge(s_bn, 1)
            act.activation(std[:, :], mv[:, :, 1], ACT.Sqrt, bias=eps_col[0:D, :]).then_inc(s_std, 1)
            with act.Fori(0, NT // K7) as i:
                for k in range(K7):
                    act.wait_ge(s_hN_p, i * K7 + (k + 1))
                    act.copy(xN[:, bass.ds(i * K7 + k, 1), :].rearrange("p a c -> p (a c)"),
                             bank[k][:, 0:D]).then_inc(s_hN_c, 1)
            act.wait_ge(s_var, 1)
            act.activation(nvar[:, :], nvar[:, :], ACT.Sqrt, bias=eps_col[:, :], scale=1.0 / D).then_inc(s_sd, 1)
            with act.Fori(0, NT // K7) as i:
                for k in range(K7):
                    act.wait_ge(s_x1_p, i * K7 + (k + 1))
                    act.copy(xT[0:D, bass.ds((i * K7 + k) * P, P)], bank[k][0:D, 0:P]).then_inc(s_x1_c, 1)
                    act.wait_ge(s_kv_p, i * K7 + (k + 1))
                    act.mul(qN[:, bass.ds(i * K7 + k, 1), :].rearrange("p a c -> p (a c)"),
                            bank[k][:, 320:320 + D], float(HD) ** -0.5).then_inc(s_q_c, 1)
            act.copy(idx[:, :, :].rearrange("p r j -> p (r j)"), src_all[:, 0:R * J]).then_inc(s_idx2, R + AHEAD)

            with act.Fori(0, TURNS) as i:
                def T_copy(r):
                    act.wait_ge(s_T, ready(i, r))
                    act.wait_ge(s_EQ, freed(i, r, 2))
                    act.copy(eaC[0:D, r % 2, :], bank[0][0:D, :])
                    act.copy(stC[:, r % 2, :], bank[1][0:W, :]).then_inc(s_tc, 1)
                    copy_indices(act, i, r, s_kvg, s_idx2)

                def exp(r):
                    act.wait_ge(s_clip, ready(i, r))
                    act.wait_ge(s_agg, freed(i, r, 2))
                    act.activation(msg[:, r % 2, :, D:DMSG], sc[:, r % 2, :].rearrange("p (j h) -> p j h", j=J),
                                   ACT.Exp).then_inc(s_exp, 1)

                T_copy(0)
                T_copy(1)
                exp(0)
                T_copy(2)
                exp(1)
                T_copy(3)
                exp(2)
                exp(3)

            with act.Fori(0, NT // K7) as i:
                for k in range(K7):
                    act.wait_ge(s_wv_p, i * K7 + (k + 1))
                    act.copy(h_stage[:, bass.ds(i * K7 + k, 1), :].rearrange("p a c -> p (a c)"),
                             bank[k][:, 0:DMSG]).then_inc(s_wv_c, 1)
            act.wait_ge(s_var, 2)
            act.activation(nvar[:, :], nvar[:, :], ACT.Sqrt, bias=eps_col[:, :], scale=1.0 / D).then_inc(s_sd, 1)

        @block.vector
        def _(dve):
            steps = [0]

            def step(ins):
                steps[0] += 1
                ins.then_inc(s_v, 1)
                dve.wait_ge(s_v, steps[0])

            for s in (s_S, s_scan, s_acc, s_S2, s_p1, s_p2, s_p3, s_clip, s_msg, s_acc2):
                dve.sem_inc(s, AHEAD)
            dve.memset(src_all[:, :], 0).then_inc(s_pads, 1)
            dve.memset(dst_i[:, :], PAD_DST).then_inc(s_pads, 1)
            dve.memset(nbr_i[:, :], PAD_DST + 1).then_inc(s_pads, 1)
            dve.memset(xT[D:DSUM, :], 1.0)
            dve.memset(eaC[D:DSUM, :, :], 1.0)
            dve.memset(last_row[0:D, :], 0.0)
            dve.memset(last_row[D:DSUM, :], 1.0)
            dve.memset(eps_col[:, :], EPS)
            dve.memset(ea[:, :, :, :], 0.0)
            dve.memset(scanE[:, :, :, D:DSUM], 0.0)
            dve.memset(scan[:, :, :], 0.0)
            dve.memset(x_stage[:, :, D:DSUM], 1.0)
            dve.memset(acc[:, 0, :], 0.0).then_inc(s_free0, 1)

            dve.wait_ge(s_dst, 48)
            dve.tensor_copy(tmpE[:, :, :], dst_i[:, :].rearrange("p (g j) -> p g j", j=J)).then_inc(s_base, 1)
            dve.wait_ge(s_base, 1)
            dve.wait_ge(s_baseP, 1)
            step(dve.tensor_scalar_min(baseB[:, :], bank[7][:, 0:NG], float(N - W)))
            dve.tensor_copy(base_i[:, :], baseB[0:1, :]).then_inc(s_base, 1)
            step(dve.tensor_tensor(rel[:, :, 0, :], tmpE[:, :, :],
                                   baseB[:, :].unsqueeze(2).to_broadcast([P, NG, J]), ALU.subtract))
            dve.wait_ge(s_prv, 48)
            step(dve.tensor_tensor(keep[:, :, :], tmpE[:, :, :], nbr_i[:, :].rearrange("p (g j) -> p g j", j=J),
                                   ALU.is_equal))
            dve.memset(nbr_i[:, :], PAD_DST + 1).then_inc(s_pads, 1)
            dve.wait_ge(s_nxt, 48)
            step(dve.tensor_tensor(tmpE[:, :, :], tmpE[:, :, :], nbr_i[:, :].rearrange("p (g j) -> p g j", j=J),
                                   ALU.not_equal))
            step(dve.scalar_tensor_tensor(out=tmpE[:, :, :], in0=rel[:, :, 0, :], scalar=1.0, in1=tmpE[:, :, :],
                                          op0=ALU.add, op1=ALU.mult))
            dve.tensor_scalar_add(rel[:, :, 1, :], tmpE[:, :, :], -1.0).then_inc(s_rel, 1)

            dve.wait_ge(s_x, 32)
            dve.tensor_copy(x_stage[:, :, 0:D], xN[:, :, :]).then_inc(s_xst, 1)
            with dve.Fori(0, NT // K7) as i:
                for k in range(K7):
                    dve.wait_ge(s_hp_p, i * K7 + (k + 1))
                    dve.tensor_scalar_max(x_stage[:, bass.ds(i * K7 + k, 1), DSUM:XROW].rearrange("p a c -> p (a c)"),
                                          bank[k][:, 128:128 + D], 0.0).then_inc(s_hp_c, 1)

            def one_hot(i, r, cols, s_used, s_made):
                dve.wait_ge(s_used, freed(i, r, 2))
                dve.tensor_tensor(S[:, r % 2, 0:cols * J, :],
                                  iotaW[:, :].unsqueeze(1).to_broadcast([P, cols * J, W]),
                                  rel[:, bass.ds(i * R + r, 1), 0:cols, :].rearrange("p a b j -> p (a b j)")
                                  .unsqueeze(2).to_broadcast([P, cols * J, W]),
                                  ALU.is_equal).then_inc(s_made, 1)

            dve.wait_ge(s_rel, 1)
            dve.memset(acc[:, 1, :], 0.0).then_inc(s_free0, 1)
            dve.wait_ge(s_free0, 2)
            dve.wait_ge(s_iden, 6)
            dve.wait_ge(s_base, 2)
            with dve.Fori(0, TURNS) as i:
                def running_max(r):
                    dve.wait_ge(s_hpT, ready(i, r))
                    dve.wait_ge(s_keepC, ready(i, r))
                    dve.wait_ge(s_back, freed(i, r, 2))
                    dve.wait_ge(s_scan, freed(i, r, 1))
                    dve.tensor_tensor_scan(out=scan[:, r % 2, :], data0=keepC[:, r % 2, :], data1=bank[r % 2][0:D, :],
                                           initial=scan[:, 1 - r % 2, GE - 1:GE], op0=ALU.mult,
                                           op1=ALU.max).then_inc(s_scan, 1)

                def add_window(r):
                    dve.wait_ge(s_max, ready(i, r))
                    dve.wait_ge(s_acc, freed(i, r, 1))
                    base = dve.value_load(base_i[0:1, bass.ds(i * R + r, 1)], min_val=0, max_val=N - W)
                    a = acc[0:DSUM, :, bass.ds(base, W)]
                    dve.tensor_tensor(a, a, bank[6 + r % 2][0:DSUM, 0:2 * W].rearrange("p (m w) -> p m w", m=2),
                                      ALU.add).then_inc(s_acc, 1)

                def front(r):
                    one_hot(i, r, 2, s_max, s_S)
                    running_max(r)

                front(0)
                front(1)
                add_window(0)
                front(2)
                add_window(1)
                front(3)
                add_window(2)
                add_window(3)

            dve.wait_ge(s_acc, NG + AHEAD)
            with dve.Fori(0, NP // CH) as i:
                dve.wait_ge(s_deg, i + 1)
                dve.tensor_scalar_max(scan[:, 0, 0:CH], bank[0][0:D, 0:CH], 1.0).then_inc(s_mean, 1)
                dve.wait_ge(s_mean, i * 3 + 1)
                dve.reciprocal(scan[:, 1, 0:CH], scan[:, 0, 0:CH]).then_inc(s_mean, 1)
                dve.wait_ge(s_mean, i * 3 + 2)
                dve.tensor_tensor(meanT[:, :], acc[0:D, 0, bass.ds(i * CH, CH)], scan[:, 1, 0:CH],
                                  ALU.mult).then_inc(s_mean, 1)

            dve.wait_ge(s_linc, NP // CH)
            with dve.Fori(0, N // BNC) as i:
                for m in range(2):
                    dve.bn_stats(stats[:, m, bass.ds(i, 1), :].rearrange("p a c -> p (a c)"),
                                 acc[0:D, m, bass.ds(i * BNC, BNC)])
            step(dve.memset(shs[:, :], 0.0))
            for m in range(2):
                last = dve.bn_aggr(mv[:, m, :], stats[:, m, :, :].rearrange("p n c -> p (n c)"))
            last.then_inc(s_bn, 1)
            dve.wait_ge(s_std, 1)
            dve.wait_ge(s_gb, 64)
            step(dve.reciprocal(rstd[:, :], std[:, :]))
            gv = gb[:, :].rearrange("p (m k) -> p m k", k=2)
            step(dve.tensor_tensor(ga[:, :], rstd[:, :], gv[:, :, 0], ALU.mult))
            step(dve.tensor_tensor(sh[:, :], ga[:, :], mv[:, :, 0], ALU.mult))
            step(dve.tensor_tensor(sh[:, :], gv[:, :, 1], sh[:, :], ALU.subtract))
            step(dve.tensor_tensor(shs[:, :], sh[:, 0:1], sh[:, 1:2], ALU.add))
            o1, o2 = acc[0:D, 0, :], acc[0:D, 1, :]
            step(dve.tensor_scalar(o1, o1, ga[:, 0:1], shs[:, :], ALU.mult, ALU.add))
            step(dve.scalar_tensor_tensor(out=o1, in0=o2, scalar=ga[:, 1:2], in1=o1, op0=ALU.mult, op1=ALU.add))
            step(dve.scalar_tensor_tensor(out=o2, in0=o1, scalar=0.01, in1=o1, op0=ALU.mult, op1=ALU.max))
            dve.tensor_tensor(o1, o2, xT[0:D, :], ALU.add).then_inc(s_hT, 1)

            def layer_norm(done):
                step(dve.reduce_sum(nmean[:, :], xN[:, :, :], AX.X))
                step(dve.tensor_scalar_mul(nmean[:, :], nmean[:, :], 1.0 / D))
                step(dve.tensor_tensor(xN[:, :, :], xN[:, :, :], nmean[:, :].unsqueeze(2).to_broadcast([P, NT, D]),
                                       ALU.subtract))
                step(dve.tensor_tensor(qN[:, :, :], xN[:, :, :], xN[:, :, :], ALU.mult))
                dve.reduce_sum(nvar[:, :], qN[:, :, :], AX.X).then_inc(s_var, 1)
                norms = 1 if done is s_x1 else 2
                dve.wait_ge(s_sd, norms)
                step(dve.reciprocal(nvar[:, :], nvar[:, :]))
                dve.tensor_tensor(xN[:, :, :], xN[:, :, :], nvar[:, :].unsqueeze(2).to_broadcast([P, NT, D]),
                                  ALU.mult).then_inc(done, 1)

            dve.wait_ge(s_hN_c, NT)
            layer_norm(s_x1)
            dve.memset(acc[:, 0, :], 0.0).then_inc(s_free0, 1)
            dve.wait_ge(s_free0, 3)
            with dve.Fori(0, NT // K7) as i:
                for k in range(K7):
                    dve.wait_ge(s_kv_p, i * K7 + (k + 1))
                    dve.wait_ge(s_q_c, i * K7 + (k + 1))
                    dve.tensor_copy(kv_stage[:, bass.ds(i * K7 + k, 1), :].rearrange("p a c -> p (a c)"),
                                    bank[k][:, 128:128 + 2 * D]).then_inc(s_kv_c, 1)

            with dve.Fori(0, TURNS) as i:
                def score(r):
                    b = r % 2
                    p3 = prod[:, b, :].rearrange("p (j c) -> p j c", j=J)
                    dve.wait_ge(s_kvg[r], i * (16 * J) + 16 * J)
                    dve.wait_ge(s_EQ, ready(i, r))
                    dve.wait_ge(s_p3, freed(i, r, 2))
                    dve.tensor_tensor(p3, kvg[:, r, :, 0:D],
                                      bank[2 + b][:, 0:J * D].rearrange("p (j c) -> p j c", j=J),
                                      ALU.mult).then_inc(s_p1, 1)
                    dve.wait_ge(s_p1, ready(i, r))
                    dve.tensor_tensor(prod[:, b, :], prod[:, b, :], bank[4 + b][:, 0:J * D],
                                      ALU.mult).then_inc(s_p2, 1)
                    dve.wait_ge(s_p2, ready(i, r))
                    dve.wait_ge(s_exp, freed(i, r, 2))
                    dve.reduce_sum(sc[:, b, :], prod[:, b, :].rearrange("p (h d) -> p h d", d=HD),
                                   AX.X).then_inc(s_p3, 1)
                    dve.wait_ge(s_p3, ready(i, r))
                    dve.tensor_scalar(sc[:, b, :], sc[:, b, :], 5.0, -5.0, ALU.min, ALU.max).then_inc(s_clip, 1)

                def message(r):
                    b = r % 2
                    dve.wait_ge(s_exp, ready(i, r))
                    dve.tensor_tensor(msg[:, b, :, 0:D].rearrange("p j (h d) -> p j h d", d=HD),
                                      kvg[:, r, :, D:2 * D].rearrange("p j (h d) -> p j h d", d=HD),
                                      msg[:, b, :, D:DMSG].unsqueeze(3).to_broadcast([P, J, H, HD]),
                                      ALU.mult).then_inc(s_msg, 1)

                def add_window(r):
                    dve.wait_ge(s_agg, ready(i, r))
                    dve.wait_ge(s_acc2, freed(i, r, 1))
                    base = dve.value_load(base_i[0:1, bass.ds(i * R + r, 1)], min_val=0, max_val=N - W)
                    a = acc[0:DMSG, 0, bass.ds(base, W)]
                    dve.tensor_tensor(a, a, bank[6 + r % 2][0:DMSG, 0:W], ALU.add).then_inc(s_acc2, 1)

                one_hot(i, 0, 1, s_agg, s_S2)
                one_hot(i, 1, 1, s_agg, s_S2)
                score(0)
                message(0)
                add_window(0)
                one_hot(i, 2, 1, s_agg, s_S2)
                score(1)
                message(1)
                add_window(1)
                one_hot(i, 3, 1, s_agg, s_S2)
                score(2)
                message(2)
                add_window(2)
                score(3)
                message(3)
                add_window(3)

            dve.wait_ge(s_wv_c, NT)
            step(dve.tensor_scalar_add(nrz[:, :, :], h_stage[:, :, D:DMSG], 1e-6))
            step(dve.reciprocal(nrz[:, :, :], nrz[:, :, :]))
            step(dve.tensor_tensor(qN[:, :, :].rearrange("p t (h d) -> p t h d", d=HD),
                                   h_stage[:, :, 0:D].rearrange("p t (h d) -> p t h d", d=HD),
                                   nrz[:, :, :].unsqueeze(3).to_broadcast([P, NT, H, HD]), ALU.mult))
            step(dve.tensor_tensor(xN[:, :, :], xN[:, :, :], qN[:, :, :], ALU.add))
            layer_norm(s_fin)

        @block.tensor
        def _(pe):
            for s in (s_hpT, s_keepP, s_sum, s_back, s_max, s_T, s_EQ, s_agg):
                pe.sem_inc(s, AHEAD)
            pe.wait_ge(s_iden, 6)
            pe.wait_ge(s_base, 1)
            pe.matmul(bank[7][:, 0:NG], first_row[:, :], tmpE[:, :, 0], start=True, stop=True).then_inc(s_baseP, 1)
            pe.wait_ge(s_x, 32)
            pe.wait_ge(s_wb, 160)
            pe.wait_ge(s_free0, 1)
            for i in range(NT // K7):
                for k in range(K7):
                    t = i * K7 + k
                    pe.transpose(bank[k][0:D, 0:P], xN[:, bass.ds(t, 1), :].rearrange("p a c -> p (a c)"),
                                 ident[:, :]).then_inc(s_xT_p, 1)
                for k in range(K7):
                    t = i * K7 + k
                    pe.wait_ge(s_xT_c, i * K7 + (k + 1))
                    pe.matmul(bank[k][:, 128:128 + D], xT[:, bass.ds(t * P, P)], w_pool[:, :],
                              start=True, stop=True).then_inc(s_hp_p, 1)
                pe.wait_ge(s_hp_c, i * K7 + K7)

            pe.wait_ge(s_rel, 1)
            with pe.Fori(0, TURNS) as i:
                def front(r):
                    b = r % 2
                    pe.wait_ge(s_gat[r], i * (16 * J) + 16 * J)
                    pe.wait_ge(s_scan, freed(i, r, 2))
                    for j in range(J):
                        last = pe.transpose(bank[b][0:D, j:GE:J], gat[:, r, j, DSUM:XROW], ident[:, :])
                    last.then_inc(s_hpT, 1)
                    pe.wait_ge(s_keepC, freed(i, r, 2))
                    for j in range(J):
                        last = pe.matmul(bank[2 + b][0:D, j:GE:J],
                                         keep[:, bass.ds(i * R + r, 1), j].to_broadcast([P, D]), identb[:, :],
                                         start=True, stop=True)
                    last.then_inc(s_keepP, 1)
                    pe.wait_ge(s_S, ready(i, r))
                    pe.wait_ge(s_acc, freed(i, r, 2))
                    for j in range(J):
                        last = pe.matmul(bank[6 + b][0:DSUM, 0:W], gat[:, r, j, 0:DSUM], S[:, b, j, :],
                                         start=j == 0, stop=j == J - 1)
                    last.then_inc(s_sum, 1)

                def back(r):
                    b = r % 2
                    pe.wait_ge(s_scan, ready(i, r))
                    pe.wait_ge(s_bcp, freed(i, r, 2))
                    for j in range(J):
                        last = pe.transpose(bank[4 + b][:, j * D:(j + 1) * D], scan[:, b, j:GE:J], ident[0:D, 0:D])
                    last.then_inc(s_back, 1)

                def ends(r):
                    b = r % 2
                    pe.wait_ge(s_bcp, ready(i, r))
                    for j in range(J):
                        last = pe.matmul(bank[6 + b][0:DSUM, W:2 * W], scanE[:, b, j, :], S[:, b, J + j, :],
                                         start=j == 0, stop=j == J - 1)
                    last.then_inc(s_max, 1)

                front(0)
                front(1)
                back(0)
                ends(0)
                front(2)
                back(1)
                ends(1)
                front(3)
                back(2)
                ends(2)
                back(3)
                ends(3)

            pe.wait_ge(s_acc, NG + AHEAD)
            pe.wait_ge(s_w, 64)
            with pe.Fori(0, NP // CH) as i:
                at = bass.ds(i * CH, CH)
                pe.matmul(bank[0][0:D, 0:CH], last_row[:, :], acc[0:DSUM, 0, at],
                          start=True, stop=True).then_inc(s_deg, 1)
                pe.wait_ge(s_mean, i * 3 + 3)
                for m, (ws, wn, agg) in enumerate(((w_self1, w_neigh1, meanT[:, :]),
                                                   (w_self2, w_neigh2, acc[0:D, 1, at]))):
                    pe.matmul(bank[1 + m][0:D, 0:CH], ws[:, :], xT[0:D, at], start=True, stop=False)
                    last = pe.matmul(bank[1 + m][0:D, 0:CH], wn[:, :], agg, start=False, stop=True)
                last.then_inc(s_lin, 1)
                pe.wait_ge(s_linc, i + 1)

            pe.wait_ge(s_hT, 1)
            for i in range(NT // K7):
                for k in range(K7):
                    pe.transpose(bank[k][:, 0:D], acc[0:D, 0, bass.ds((i * K7 + k) * P, P)],
                                 ident[0:D, 0:D]).then_inc(s_hN_p, 1)
                pe.wait_ge(s_hN_c, i * K7 + K7)

            pe.wait_ge(s_x1, 1)
            for i in range(NT // K7):
                for k in range(K7):
                    pe.transpose(bank[k][0:D, 0:P], xN[:, bass.ds(i * K7 + k, 1), :].rearrange("p a c -> p (a c)"),
                                 ident[:, :]).then_inc(s_x1_p, 1)
                for k in range(K7):
                    at = bass.ds((i * K7 + k) * P, P)
                    pe.wait_ge(s_x1_c, i * K7 + (k + 1))
                    pe.matmul(bank[k][:, 128:128 + 2 * D], xT[:, at], w_kv[:, :], start=True, stop=True)
                    pe.matmul(bank[k][:, 320:320 + D], xT[:, at], w_q[:, :], start=True,
                              stop=True).then_inc(s_kv_p, 1)
                pe.wait_ge(s_kv_c, i * K7 + K7)
                pe.wait_ge(s_q_c, i * K7 + K7)

            with pe.Fori(0, TURNS) as i:
                def transposes(r):
                    b = r % 2
                    pe.wait_ge(s_ea[r], i * 16 + 16)
                    pe.wait_ge(s_tc, freed(i, r, 1))
                    pe.wait_ge(s_S2, ready(i, r))
                    for j in range(J):
                        pe.transpose(bank[0][0:D, j * P:(j + 1) * P], ea[:, r, j, :], ident[:, :])
                    for j in range(J):
                        last = pe.transpose(bank[1][0:W, j * P:(j + 1) * P], S[:, b, j, :], ident[:, :])
                    last.then_inc(s_T, 1)

                def expand(r):
                    b = r % 2
                    pe.wait_ge(s_tc, ready(i, r))
                    pe.wait_ge(s_qw[r], i * 16 + 16)
                    pe.wait_ge(s_p2, freed(i, r, 2))
                    for j in range(J):
                        pe.matmul(bank[2 + b][:, j * D:(j + 1) * D], eaC[:, b, j * P:(j + 1) * P], w_e[:, :],
                                  start=True, stop=True)
                    for j in range(J):
                        last = pe.matmul(bank[4 + b][:, j * D:(j + 1) * D], stC[:, b, j * P:(j + 1) * P],
                                         qwin[:, r, :], start=True, stop=True)
                    last.then_inc(s_EQ, 1)

                def aggregate(r):
                    b = r % 2
                    pe.wait_ge(s_msg, ready(i, r))
                    pe.wait_ge(s_acc2, freed(i, r, 2))
                    for j in range(J):
                        last = pe.matmul(bank[6 + b][0:DMSG, 0:W], msg[:, b, j, :], S[:, b, j, :],
                                         start=j == 0, stop=j == J - 1)
                    last.then_inc(s_agg, 1)

                transposes(0)
                transposes(1)
                expand(0)
                expand(1)
                aggregate(0)
                transposes(2)
                expand(2)
                aggregate(1)
                transposes(3)
                expand(3)
                aggregate(2)
                aggregate(3)

            pe.wait_ge(s_acc2, NG + AHEAD)
            for i in range(NT // K7):
                for k in range(K7):
                    pe.transpose(bank[k][:, 0:DMSG], acc[0:DMSG, 0, bass.ds((i * K7 + k) * P, P)],
                                 ident[0:DMSG, 0:DMSG]).then_inc(s_wv_p, 1)
                pe.wait_ge(s_wv_c, i * K7 + K7)


_WEIGHTS = ['L0_gnn_W_self1', 'L0_gnn_W_neigh1', 'L0_gnn_W_pool', 'L0_gnn_b_pool', 'L0_gnn_W_self2', 'L0_gnn_W_neigh2',
            'L0_gnn_g1', 'L0_gnn_beta1', 'L0_gnn_g2', 'L0_gnn_beta2', 'L1_gnn_Wq', 'L1_gnn_bq', 'L1_gnn_Wk',
            'L1_gnn_bk', 'L1_gnn_We', 'L1_gnn_be', 'L1_gnn_Wv', 'L1_gnn_bv']


def kernel(**inputs):
    import numpy as _np
    import concourse.bacc as _bacc
    from concourse import mybir as _mybir
    from concourse.bass_utils import run_bass_kernel_spmd as _run

    def split(a):
        whole = a[:FULL * GE].reshape(FULL, P, J).transpose(1, 0, 2).reshape(P, FULL * J)
        return _np.ascontiguousarray(whole), _np.ascontiguousarray(a[FULL * GE:])

    src, dst = _np.asarray(inputs['src']), _np.asarray(inputs['dst'])
    named = [('x', inputs['x'])]
    for name, a in (('src', src), ('dst', dst), ('before', _np.concatenate([dst[:1], dst[:-1]])), ('after', dst[1:])):
        whole, rest = split(a)
        named += [(name + '_groups', whole), (name + '_rest', rest)]
    named += [('edge_attr', inputs['edge_attr_96'])] + [(n, inputs[n]) for n in _WEIGHTS]
    nc = _bacc.Bacc("TRN2", target_bir_lowering=False, num_devices=1)
    arrays, args = {}, []
    for name, a in named:
        a = _np.ascontiguousarray(a)
        arrays[f"in_{name}_dram"] = a
        args.append(nc.dram_tensor(f"in_{name}_dram", a.shape, _mybir.dt.from_np(a.dtype), kind="ExternalInput").ap())
    args.append(nc.dram_tensor("out_0_dram", (N, D), _mybir.dt.float32, kind="ExternalOutput").ap())
    build(nc, *args)
    return _run(nc, [arrays], core_ids=[0]).results[0]["out_0_dram"]
```

```python
import concourse.bass as bass
from concourse import mybir
from contextlib import ExitStack

F32 = mybir.dt.float32
BF16 = mybir.dt.bfloat16
I32 = mybir.dt.int32
ALU = mybir.AluOpType
ACT = mybir.ActivationFunctionType
AX = mybir.AxisListType

N, D, E = 6250, 96, 206250
H = 8
HD = D // H
P = 128
J = 4
GE = P * J
FULL = E // GE
TAIL = E - FULL * GE
R = 4
TURNS = -(-(FULL + 1) // R)
NG = TURNS * R
W = 64
NT = -(-N // P)
NFULL = N // P
NTAIL = N - NFULL * P
NP = NT * P
K7 = 7
CH = NP // 14
BNC = 250
XROW = 2 * D + 1
DSUM = D + 1
DMSG = D + H
PAD_DST = 20000
EPS = 1e-5
AHEAD = 4


def build(nc, x, src_m, src_t, dst_m, dst_t, prv_m, prv_t, nxt_m, nxt_t, edge_attr, Ws1, Wn1, Wp, bp, Ws2, Wn2,
          g1, be1, g2, be2, Wq, bq, Wk, bk, We, be, Wv, bv, out):
    ctx = ExitStack()
    with ctx:
        def sb(name, shape, dt=F32):
            return ctx.enter_context(nc.sbuf_tensor(name, shape, dt))

        def sem(name):
            return ctx.enter_context(nc.semaphore(name))

        x_table = nc.dram_tensor("x_table", (NP, XROW), F32, kind="Internal").ap()
        kv_table = nc.dram_tensor("kv_table", (NP, 2 * D), F32, kind="Internal").ap()
        q_table = nc.dram_tensor("q_table", (NP, D), F32, kind="Internal").ap()

        xN = sb("xN", [P, NT, D])
        stage = sb("stage", [P, NT * XROW])
        xT = sb("xT", [DSUM, NP])
        acc = sb("acc", [P, 2, NP])
        qN = acc[:, 1, 0:NT * D].rearrange("p (t c) -> p t c", t=NT)
        dst_i = acc[:, 1, 0:NG * J].bitcast(I32)
        nbr_i = acc[:, 1, NG * J:2 * NG * J].bitcast(I32)
        tmpE = acc[:, 1, 2 * NG * J:3 * NG * J].rearrange("p (g j) -> p g j", j=J)
        x_stage = stage[:, :].rearrange("p (t c) -> p t c", t=NT)
        kv_stage = stage[:, 0:NT * 2 * D].rearrange("p (t c) -> p t c", t=NT)
        h_stage = stage[:, 0:NT * DMSG].rearrange("p (t c) -> p t c", t=NT)

        src_all = sb("src_all", [P, (NG + R) * J], I32)
        rel = sb("rel", [P, NG, 2, J])
        keep = sb("keep", [P, NG, J], BF16)
        base_i = sb("base_i", [1, NG], I32)
        idx = sb("idx", [P, R, J], I32)

        gat = sb("gat", [P, R, J, XROW])
        kvg = gat[:, :, :, 0:2 * D]
        S = sb("S", [P, R, 2 * J, W])
        baseB = S[:, 0, :, :].rearrange("p j w -> p (j w)")[:, 0:NG]
        keepC = sb("keepC", [D, 2, GE], BF16)
        scan = sb("scan", [D, 2, GE])
        scanE = sb("scanE", [P, 2, J, DSUM])
        ea = sb("ea", [P, R, J, D])
        qwin = sb("qwin", [W, R, D])
        eaC = sb("eaC", [DSUM, 2, GE])
        stC = scan[0:W, :, :]
        prod = sb("prod", [P, 2, J * D])
        sc = sb("sc", [P, 2, J * H])
        msg = sb("msg", [P, 2, J, DMSG])

        ident = sb("ident", [P, P])
        identb = sb("identb", [P, P], BF16)
        first_row = sb("first_row", [P, P])
        last_row = sb("last_row", [DSUM, D])
        iotaW = sb("iotaW", [P, W])
        w_self1 = sb("w_self1", [D, D])
        w_neigh1 = sb("w_neigh1", [D, D])
        w_self2 = sb("w_self2", [D, D])
        w_neigh2 = sb("w_neigh2", [D, D])
        w_pool = sb("w_pool", [DSUM, D])
        w_kv = sb("w_kv", [DSUM, 2 * D])
        w_q = sb("w_q", [DSUM, D])
        w_e = sb("w_e", [DSUM, D])
        gb = sb("gb", [D, 4])
        eps_col = sb("eps_col", [P, 1])
        meanT = prod[0:D, :, :].rearrange("p b c -> p (b c)")[:, 0:CH]
        stats = sb("stats", [D, 2, N // BNC, 6])
        mv = sb("mv", [D, 2, 2])
        std = sb("std", [D, 2])
        rstd = sb("rstd", [D, 2])
        ga = sb("ga", [D, 2])
        sh = sb("sh", [D, 2])
        shs = sb("shs", [D, 1])
        nmean = sb("nmean", [P, NT])
        nvar = sb("nvar", [P, NT])
        nrz = prod[:, :, :].rearrange("p b c -> p (b c)")[:, 0:NT * H].rearrange("p (t h) -> p t h", t=NT)

        bank = [ctx.enter_context(nc.psum_tensor(f"bank{k}", [P, 512], F32)) for k in range(8)]

        s_x, s_w, s_wb, s_gb = sem("s_x"), sem("s_w"), sem("s_wb"), sem("s_gb")
        s_src, s_dst, s_prv, s_nxt = sem("s_src"), sem("s_dst"), sem("s_prv"), sem("s_nxt")
        s_xtab, s_kvtab, s_out = sem("s_xtab"), sem("s_kvtab"), sem("s_out")
        s_gat = [sem(f"s_gat{r}") for r in range(R)]
        s_kvg = [sem(f"s_kvg{r}") for r in range(R)]
        s_ea = [sem(f"s_ea{r}") for r in range(R)]
        s_qw = [sem(f"s_qw{r}") for r in range(R)]
        s_tail = sem("s_tail")
        s_zero, s_pads, s_iden = sem("s_zero"), sem("s_pads"), sem("s_iden")
        s_v = sem("s_v")
        s_base, s_baseP, s_rel = sem("s_base"), sem("s_baseP"), sem("s_rel")
        s_xT_p, s_xT_c, s_hp_p, s_hp_c = sem("s_xT_p"), sem("s_xT_c"), sem("s_hp_p"), sem("s_hp_c")
        s_xst = sem("s_xst")
        s_idx, s_free0, s_S, s_hpT, s_keepP, s_keepC = (sem("s_idx"), sem("s_free0"), sem("s_S"), sem("s_hpT"),
                                                        sem("s_keepP"), sem("s_keepC"))
        s_sum, s_scan, s_back, s_bcp, s_max, s_acc = (sem("s_sum"), sem("s_scan"), sem("s_back"), sem("s_bcp"),
                                                      sem("s_max"), sem("s_acc"))
        s_deg, s_mean, s_lin, s_linc, s_bn, s_std = (sem("s_deg"), sem("s_mean"), sem("s_lin"), sem("s_linc"),
                                                     sem("s_bn"), sem("s_std"))
        s_hT, s_hN_p, s_hN_c, s_var, s_sd, s_x1 = (sem("s_hT"), sem("s_hN_p"), sem("s_hN_c"), sem("s_var"),
                                                   sem("s_sd"), sem("s_x1"))
        s_x1_p, s_x1_c, s_kv_p, s_kv_c, s_q_c = (sem("s_x1_p"), sem("s_x1_c"), sem("s_kv_p"), sem("s_kv_c"),
                                                 sem("s_q_c"))
        s_idx2, s_S2, s_T, s_tc, s_EQ = sem("s_idx2"), sem("s_S2"), sem("s_T"), sem("s_tc"), sem("s_EQ")
        s_p1, s_p2, s_p3, s_clip, s_exp = sem("s_p1"), sem("s_p2"), sem("s_p3"), sem("s_clip"), sem("s_exp")
        s_msg, s_agg, s_acc2 = sem("s_msg"), sem("s_agg"), sem("s_acc2")
        s_wv_p, s_wv_c, s_fin, s_tick = sem("s_wv_p"), sem("s_wv_c"), sem("s_fin"), sem("s_tick")

        def ready(i, r):
            return i * R + (r + 1 + AHEAD)

        def freed(i, r, depth):
            return i * R + (r + 1 + AHEAD - depth)

        def landed(i, r, per_turn):
            return (i + r // R) * per_turn + per_turn

        def pipeline(eng, turn, lag):
            turn(0, range(R), lambda r: r >= 0)
            with eng.Fori(1, TURNS) as i:
                turn(i, range(R), lambda r: True)
            turn(TURNS, range(lag), lambda r: r < 0)

        block = ctx.enter_context(nc.Block())

        @block.sync
        def _(sp):
            sp.wait_ge(s_zero, 1)
            sp.dma_start(xN[:, 0:NFULL, :], x[0:NFULL * P, :].rearrange("(t p) c -> p t c", p=P)).then_inc(s_x, 16)
            sp.dma_start(xN[0:NTAIL, NFULL, :], x[NFULL * P:N, :]).then_inc(s_x, 16)
            for w, v in ((w_self1, Ws1), (w_neigh1, Wn1), (w_self2, Ws2), (w_neigh2, Wn2)):
                sp.dma_start(w[:, :], v[:, :]).then_inc(s_w, 16)
            for w, v, b in ((w_pool[:, :], Wp, bp), (w_kv[:, 0:D], Wk, bk), (w_kv[:, D:2 * D], Wv, bv),
                            (w_q[:, :], Wq, bq), (w_e[:, :], We, be)):
                sp.dma_start(w[0:D, :], v[:, :]).then_inc(s_wb, 16)
                sp.dma_start(w[D:D + 1, :], b.rearrange("(a c) -> a c", a=1)).then_inc(s_wb, 16)
            with nc.allow_non_contiguous_dma(reason="four columns of 96 numbers"):
                for n, v in enumerate((g1, be1, g2, be2)):
                    sp.dma_start(gb[:, n:n + 1], v.rearrange("(c a) -> c a", a=1)).then_inc(s_gb, 16)

            def edges(to, main, tail, done):
                n = tail.shape[0]
                sp.dma_start(to[:, 0:FULL * J], main).then_inc(done, 16)
                sp.dma_start(to[0:n // J, FULL * J:(FULL + 1) * J],
                             tail[0:n // J * J].rearrange("(p j) -> p j", j=J)).then_inc(done, 16)
                sp.dma_start(to[n // J:n // J + 1, FULL * J:FULL * J + n % J],
                             tail[n // J * J:n].rearrange("(a j) -> a j", a=1)).then_inc(done, 16)

            sp.wait_ge(s_pads, 3)
            edges(src_all, src_m, src_t, s_src)
            edges(dst_i, dst_m, dst_t, s_dst)
            edges(nbr_i, prv_m, prv_t, s_prv)
            sp.wait_ge(s_pads, 4)
            edges(nbr_i, nxt_m, nxt_t, s_nxt)
            sp.wait_ge(s_xst, 1)
            sp.wait_ge(s_hp_c, NT)
            sp.dma_start(x_table.rearrange("(t p) c -> p t c", p=P), x_stage).then_inc(s_xtab, 16)

            sp.wait_ge(s_kv_c, NT)
            sp.wait_ge(s_q_c, NT)
            sp.dma_start(kv_table.rearrange("(t p) c -> p t c", p=P), kv_stage).then_inc(s_kvtab, 16)
            sp.dma_start(q_table.rearrange("(t p) c -> p t c", p=P), qN[:, :, :]).then_inc(s_kvtab, 16)
            sp.wait_ge(s_kvtab, 32)

            ea_v = edge_attr[0:FULL * GE, :].rearrange("(g p j) c -> p g (j c)", p=P, j=J)

            def load_group(i, r, ea_src):
                sp.wait_ge(s_T, freed(i, r, R))
                if ea_src is not None:
                    ea_src()
                sp.wait_ge(s_EQ, freed(i, r, R))
                base = sp.value_load(base_i[0:1, bass.ds(i * R + r, 1)], min_val=0, max_val=N - W)
                sp.dma_start(qwin[:, r, :], q_table[bass.ds(base, W), :]).then_inc(s_qw[r], 16)

            with sp.Fori(0, FULL // R) as i:
                for r in range(R):
                    load_group(i, r, lambda: sp.dma_start(
                        ea[:, r, :, :].rearrange("p j c -> p (j c)"),
                        ea_v[:, bass.ds(i * R + r, 1), :].rearrange("p g c -> p (g c)")).then_inc(s_ea[r], 16))

            def tail_load(g, r):
                if g < FULL:
                    sp.dma_start(ea[:, r, :, :].rearrange("p j c -> p (j c)"), ea_v[:, g, :]).then_inc(s_ea[r], 16)
                elif g == FULL:
                    e0, whole = FULL * GE, TAIL // J
                    sp.dma_start(ea[0:whole, r, :, :].rearrange("p j c -> p (j c)"),
                                 edge_attr[e0:e0 + whole * J, :].rearrange("(p j) c -> p (j c)", j=J)
                                 ).then_inc(s_tail, 16)
                    sp.wait_ge(s_tail, 16)
                    sp.dma_start(ea[whole:whole + 1, r, 0:TAIL % J, :].rearrange("p j c -> p (j c)"),
                                 edge_attr[e0 + whole * J:E, :].rearrange("(a j) c -> a (j c)", a=1)
                                 ).then_inc(s_ea[r], 16)
                else:
                    sp.sem_inc(s_ea[r], 16)

            for g in range(FULL // R * R, NG):
                load_group(g // R, g % R, lambda: tail_load(g, g % R))

            sp.wait_ge(s_fin, 1)
            sp.dma_start(out[0:NFULL * P, :].rearrange("(t p) c -> p t c", p=P), xN[:, 0:NFULL, :]).then_inc(s_out, 16)
            sp.dma_start(out[NFULL * P:N, :], xN[0:NTAIL, NFULL, :]).then_inc(s_out, 16)
            sp.wait_ge(s_out, 32)

        @block.gpsimd
        def _(pool):
            pool.memset(xN[:, NFULL, :], 0.0).then_inc(s_zero, 1)
            pool.memset(ident[:, :], 0.0).then_inc(s_iden, 1)
            pool.memset(first_row[:, :], 1.0).then_inc(s_iden, 1)
            pool.iota(iotaW[:, :], pattern=[[1, W]], base=0, channel_multiplier=0,
                      allow_small_or_imprecise_dtypes=True).then_inc(s_iden, 1)
            pool.wait_ge(s_iden, 3)
            pool.affine_select(out=ident[:, :], in_=ident[:, :], compare_op=ALU.not_equal, fill=1.0, base=0,
                               pattern=[[-1, P]], channel_multiplier=1).then_inc(s_iden, 1)
            pool.affine_select(out=first_row[:, :], in_=first_row[:, :], compare_op=ALU.is_equal, fill=0.0, base=0,
                               pattern=[[0, P]], channel_multiplier=1).then_inc(s_iden, 1)
            pool.wait_ge(s_iden, 5)
            pool.tensor_copy(identb[:, :], ident[:, :]).then_inc(s_iden, 1)

            def gathers(table, width, s_i, s_free, s_done, turn_of):
                with pool.Fori(0, TURNS) as i:
                    for r in range(R):
                        pool.wait_ge(s_i, ready(i, r))
                        pool.sem_inc(s_tick, 1)
                        pool.wait_ge(s_free, freed(i, r, R))
                        pool.sem_inc(s_tick, 1)
                        for j in range(J):
                            pool.indirect_dma_start(
                                out=gat[:, r, j, 0:width], out_offset=None, in_=table,
                                in_offset=bass.IndirectOffsetOnAxis(ap=idx[:, r, j:j + 1], axis=0)
                            ).then_inc(s_done[r], 16)

            pool.wait_ge(s_xtab, 16)
            gathers(x_table, XROW, s_idx, s_sum, s_gat, None)
            pool.wait_ge(s_kvtab, 32)
            gathers(kv_table, 2 * D, s_idx2, s_msg, s_kvg, None)

        def copy_indices(act, i, r, s_done, s_i):
            act.wait_ge(s_done[r % R], landed(i, r, 16 * J))
            act.copy(idx[:, r % R, :], src_all[:, bass.ds((i * R + (r + R)) * J, J)]).then_inc(s_i, 1)

        @block.scalar
        def _(act):
            for s in (s_keepC, s_bcp, s_tc, s_exp):
                act.sem_inc(s, AHEAD)
            with act.Fori(0, NT // K7) as i:
                for k in range(K7):
                    act.wait_ge(s_xT_p, i * K7 + (k + 1))
                    act.copy(xT[0:D, bass.ds((i * K7 + k) * P, P)], bank[k][0:D, 0:P]).then_inc(s_xT_c, 1)
            act.wait_ge(s_src, 48)
            act.copy(idx[:, :, :].rearrange("p r j -> p (r j)"), src_all[:, 0:R * J]).then_inc(s_idx, R + AHEAD)

            def turn1(i, steps, live):
                def keep_copy(r):
                    copy_indices(act, i, r, s_gat, s_idx)
                    act.wait_ge(s_keepP, ready(i, r))
                    act.wait_ge(s_scan, freed(i, r, 2))
                    act.copy(keepC[:, r % 2, :], bank[2 + r % 2][0:D, :]).then_inc(s_keepC, 1)

                def back_copy(r):
                    act.wait_ge(s_back, ready(i, r))
                    act.wait_ge(s_max, freed(i, r, 2))
                    act.copy(scanE[:, r % 2, :, 0:D],
                             bank[4 + r % 2][:, 0:J * D].rearrange("p (j c) -> p j c", j=J)).then_inc(s_bcp, 1)

                for r in steps:
                    if live(r):
                        keep_copy(r)
                    if live(r - 1):
                        back_copy(r - 1)

            pipeline(act, turn1, 1)

            with act.Fori(0, NP // CH) as i:
                act.wait_ge(s_lin, i + 1)
                for m in range(2):
                    last = act.copy(acc[0:D, m, bass.ds(i * CH, CH)], bank[1 + m][0:D, 0:CH])
                last.then_inc(s_linc, 1)
            act.wait_ge(s_bn, 1)
            act.activation(std[:, :], mv[:, :, 1], ACT.Sqrt, bias=eps_col[0:D, :]).then_inc(s_std, 1)
            with act.Fori(0, NT // K7) as i:
                for k in range(K7):
                    act.wait_ge(s_hN_p, i * K7 + (k + 1))
                    act.copy(xN[:, bass.ds(i * K7 + k, 1), :].rearrange("p a c -> p (a c)"),
                             bank[k][:, 0:D]).then_inc(s_hN_c, 1)
            act.wait_ge(s_var, 1)
            act.activation(nvar[:, :], nvar[:, :], ACT.Sqrt, bias=eps_col[:, :], scale=1.0 / D).then_inc(s_sd, 1)
            with act.Fori(0, NT // K7) as i:
                for k in range(K7):
                    act.wait_ge(s_x1_p, i * K7 + (k + 1))
                    act.copy(xT[0:D, bass.ds((i * K7 + k) * P, P)], bank[k][0:D, 0:P]).then_inc(s_x1_c, 1)
                    act.wait_ge(s_kv_p, i * K7 + (k + 1))
                    act.mul(qN[:, bass.ds(i * K7 + k, 1), :].rearrange("p a c -> p (a c)"),
                            bank[k][:, 320:320 + D], float(HD) ** -0.5).then_inc(s_q_c, 1)
            act.copy(idx[:, :, :].rearrange("p r j -> p (r j)"), src_all[:, 0:R * J]).then_inc(s_idx2, R + AHEAD)

            def turn2(i, steps, live):
                def T_copy(r):
                    act.wait_ge(s_T, ready(i, r))
                    act.wait_ge(s_EQ, freed(i, r, 2))
                    act.copy(eaC[0:D, r % 2, :], bank[0][0:D, :])
                    act.copy(stC[:, r % 2, :], bank[1][0:W, :]).then_inc(s_tc, 1)

                def exp(r):
                    act.wait_ge(s_clip, ready(i, r))
                    act.wait_ge(s_agg, freed(i, r, 2))
                    act.activation(msg[:, r % 2, :, D:DMSG], sc[:, r % 2, :].rearrange("p (j h) -> p j h", j=J),
                                   ACT.Exp).then_inc(s_exp, 1)

                for r in steps:
                    if live(r):
                        T_copy(r)
                    if live(r - 2):
                        copy_indices(act, i, r - 2, s_kvg, s_idx2)
                        exp(r - 2)

            pipeline(act, turn2, 2)

            with act.Fori(0, NT // K7) as i:
                for k in range(K7):
                    act.wait_ge(s_wv_p, i * K7 + (k + 1))
                    act.copy(h_stage[:, bass.ds(i * K7 + k, 1), :].rearrange("p a c -> p (a c)"),
                             bank[k][:, 0:DMSG]).then_inc(s_wv_c, 1)
            act.wait_ge(s_var, 2)
            act.activation(nvar[:, :], nvar[:, :], ACT.Sqrt, bias=eps_col[:, :], scale=1.0 / D).then_inc(s_sd, 1)

        @block.vector
        def _(dve):
            steps = [0]

            def step(ins):
                steps[0] += 1
                ins.then_inc(s_v, 1)
                dve.wait_ge(s_v, steps[0])

            for s in (s_S, s_scan, s_acc, s_S2, s_p1, s_p2, s_p3, s_clip, s_msg, s_acc2):
                dve.sem_inc(s, AHEAD)
            dve.memset(src_all[:, :], 0).then_inc(s_pads, 1)
            dve.memset(dst_i[:, :], PAD_DST).then_inc(s_pads, 1)
            dve.memset(nbr_i[:, :], PAD_DST + 1).then_inc(s_pads, 1)
            dve.memset(xT[D:DSUM, :], 1.0)
            dve.memset(eaC[D:DSUM, :, :], 1.0)
            dve.memset(last_row[0:D, :], 0.0)
            dve.memset(last_row[D:DSUM, :], 1.0)
            dve.memset(eps_col[:, :], EPS)
            dve.memset(ea[:, :, :, :], 0.0)
            dve.memset(scanE[:, :, :, D:DSUM], 0.0)
            dve.memset(scan[:, :, :], 0.0)
            dve.memset(x_stage[:, :, D:DSUM], 1.0)
            dve.memset(acc[:, 0, :], 0.0).then_inc(s_free0, 1)

            dve.wait_ge(s_dst, 48)
            dve.tensor_copy(tmpE[:, :, :], dst_i[:, :].rearrange("p (g j) -> p g j", j=J)).then_inc(s_base, 1)
            dve.wait_ge(s_base, 1)
            dve.wait_ge(s_baseP, 1)
            step(dve.tensor_scalar_min(baseB[:, :], bank[7][:, 0:NG], float(N - W)))
            dve.tensor_copy(base_i[:, :], baseB[0:1, :]).then_inc(s_base, 1)
            step(dve.tensor_tensor(rel[:, :, 0, :], tmpE[:, :, :],
                                   baseB[:, :].unsqueeze(2).to_broadcast([P, NG, J]), ALU.subtract))
            dve.wait_ge(s_prv, 48)
            step(dve.tensor_tensor(keep[:, :, :], tmpE[:, :, :], nbr_i[:, :].rearrange("p (g j) -> p g j", j=J),
                                   ALU.is_equal))
            dve.memset(nbr_i[:, :], PAD_DST + 1).then_inc(s_pads, 1)
            dve.wait_ge(s_nxt, 48)
            step(dve.tensor_tensor(tmpE[:, :, :], tmpE[:, :, :], nbr_i[:, :].rearrange("p (g j) -> p g j", j=J),
                                   ALU.not_equal))
            step(dve.scalar_tensor_tensor(out=tmpE[:, :, :], in0=rel[:, :, 0, :], scalar=1.0, in1=tmpE[:, :, :],
                                          op0=ALU.add, op1=ALU.mult))
            dve.tensor_scalar_add(rel[:, :, 1, :], tmpE[:, :, :], -1.0).then_inc(s_rel, 1)

            dve.wait_ge(s_x, 32)
            dve.tensor_copy(x_stage[:, :, 0:D], xN[:, :, :]).then_inc(s_xst, 1)
            with dve.Fori(0, NT // K7) as i:
                for k in range(K7):
                    dve.wait_ge(s_hp_p, i * K7 + (k + 1))
                    dve.tensor_scalar_max(x_stage[:, bass.ds(i * K7 + k, 1), DSUM:XROW].rearrange("p a c -> p (a c)"),
                                          bank[k][:, 128:128 + D], 0.0).then_inc(s_hp_c, 1)

            def one_hot(i, r, cols, s_used, s_made):
                dve.wait_ge(s_used, freed(i, r, R))
                dve.tensor_tensor(S[:, r % R, 0:cols * J, :], iotaW[:, :].unsqueeze(1).to_broadcast([P, cols * J, W]),
                                  rel[:, bass.ds(i * R + r, 1), 0:cols, :].rearrange("p a b j -> p (a b j)")
                                  .unsqueeze(2).to_broadcast([P, cols * J, W]),
                                  ALU.is_equal).then_inc(s_made, 1)

            dve.wait_ge(s_rel, 1)
            dve.memset(acc[:, 1, :], 0.0).then_inc(s_free0, 1)
            dve.wait_ge(s_free0, 2)
            dve.wait_ge(s_iden, 6)
            dve.wait_ge(s_base, 2)
            def turn1(i, steps, live):
                def running_max(r):
                    dve.wait_ge(s_hpT, ready(i, r))
                    dve.wait_ge(s_keepC, ready(i, r))
                    dve.wait_ge(s_back, freed(i, r, 2))
                    dve.wait_ge(s_scan, freed(i, r, 1))
                    dve.tensor_tensor_scan(out=scan[:, r % 2, :], data0=keepC[:, r % 2, :], data1=bank[r % 2][0:D, :],
                                           initial=scan[:, (r + 1) % 2, GE - 1:GE], op0=ALU.mult,
                                           op1=ALU.max).then_inc(s_scan, 1)

                def add_window(r):
                    dve.wait_ge(s_max, ready(i, r))
                    dve.wait_ge(s_acc, freed(i, r, 1))
                    base = dve.value_load(base_i[0:1, bass.ds(i * R + r, 1)], min_val=0, max_val=N - W)
                    a = acc[0:DSUM, :, bass.ds(base, W)]
                    dve.tensor_tensor(a, a, bank[6 + r % 2][0:DSUM, 0:2 * W].rearrange("p (m w) -> p m w", m=2),
                                      ALU.add).then_inc(s_acc, 1)

                for r in steps:
                    if live(r):
                        one_hot(i, r, 2, s_max, s_S)
                    if live(r - 1):
                        running_max(r - 1)
                    if live(r - 2):
                        add_window(r - 2)

            pipeline(dve, turn1, 2)

            dve.wait_ge(s_acc, NG + AHEAD)
            with dve.Fori(0, NP // CH) as i:
                dve.wait_ge(s_deg, i + 1)
                dve.tensor_scalar_max(scan[:, 0, 0:CH], bank[0][0:D, 0:CH], 1.0).then_inc(s_mean, 1)
                dve.wait_ge(s_mean, i * 3 + 1)
                dve.reciprocal(scan[:, 1, 0:CH], scan[:, 0, 0:CH]).then_inc(s_mean, 1)
                dve.wait_ge(s_mean, i * 3 + 2)
                dve.tensor_tensor(meanT[:, :], acc[0:D, 0, bass.ds(i * CH, CH)], scan[:, 1, 0:CH],
                                  ALU.mult).then_inc(s_mean, 1)

            dve.wait_ge(s_linc, NP // CH)
            with dve.Fori(0, N // BNC) as i:
                for m in range(2):
                    dve.bn_stats(stats[:, m, bass.ds(i, 1), :].rearrange("p a c -> p (a c)"),
                                 acc[0:D, m, bass.ds(i * BNC, BNC)])
            step(dve.memset(shs[:, :], 0.0))
            for m in range(2):
                last = dve.bn_aggr(mv[:, m, :], stats[:, m, :, :].rearrange("p n c -> p (n c)"))
            last.then_inc(s_bn, 1)
            dve.wait_ge(s_std, 1)
            dve.wait_ge(s_gb, 64)
            step(dve.reciprocal(rstd[:, :], std[:, :]))
            gv = gb[:, :].rearrange("p (m k) -> p m k", k=2)
            step(dve.tensor_tensor(ga[:, :], rstd[:, :], gv[:, :, 0], ALU.mult))
            step(dve.tensor_tensor(sh[:, :], ga[:, :], mv[:, :, 0], ALU.mult))
            step(dve.tensor_tensor(sh[:, :], gv[:, :, 1], sh[:, :], ALU.subtract))
            step(dve.tensor_tensor(shs[:, :], sh[:, 0:1], sh[:, 1:2], ALU.add))
            o1, o2 = acc[0:D, 0, :], acc[0:D, 1, :]
            step(dve.tensor_scalar(o1, o1, ga[:, 0:1], shs[:, :], ALU.mult, ALU.add))
            step(dve.scalar_tensor_tensor(out=o1, in0=o2, scalar=ga[:, 1:2], in1=o1, op0=ALU.mult, op1=ALU.add))
            step(dve.scalar_tensor_tensor(out=o2, in0=o1, scalar=0.01, in1=o1, op0=ALU.mult, op1=ALU.max))
            dve.tensor_tensor(o1, o2, xT[0:D, :], ALU.add).then_inc(s_hT, 1)

            def layer_norm(done):
                step(dve.reduce_sum(nmean[:, :], xN[:, :, :], AX.X))
                step(dve.tensor_scalar_mul(nmean[:, :], nmean[:, :], 1.0 / D))
                step(dve.tensor_tensor(xN[:, :, :], xN[:, :, :], nmean[:, :].unsqueeze(2).to_broadcast([P, NT, D]),
                                       ALU.subtract))
                step(dve.tensor_tensor(qN[:, :, :], xN[:, :, :], xN[:, :, :], ALU.mult))
                dve.reduce_sum(nvar[:, :], qN[:, :, :], AX.X).then_inc(s_var, 1)
                norms = 1 if done is s_x1 else 2
                dve.wait_ge(s_sd, norms)
                step(dve.reciprocal(nvar[:, :], nvar[:, :]))
                dve.tensor_tensor(xN[:, :, :], xN[:, :, :], nvar[:, :].unsqueeze(2).to_broadcast([P, NT, D]),
                                  ALU.mult).then_inc(done, 1)

            dve.wait_ge(s_hN_c, NT)
            layer_norm(s_x1)
            dve.memset(acc[:, 0, :], 0.0).then_inc(s_free0, 1)
            dve.wait_ge(s_free0, 3)
            with dve.Fori(0, NT // K7) as i:
                for k in range(K7):
                    dve.wait_ge(s_kv_p, i * K7 + (k + 1))
                    dve.wait_ge(s_q_c, i * K7 + (k + 1))
                    dve.tensor_copy(kv_stage[:, bass.ds(i * K7 + k, 1), :].rearrange("p a c -> p (a c)"),
                                    bank[k][:, 128:128 + 2 * D]).then_inc(s_kv_c, 1)

            def turn2(i, steps, live):
                def products_e(r):
                    b = r % 2
                    dve.wait_ge(s_kvg[r % R], landed(i, r, 16 * J))
                    dve.wait_ge(s_EQ, ready(i, r))
                    dve.wait_ge(s_p3, freed(i, r, 2))
                    dve.tensor_tensor(prod[:, b, :].rearrange("p (j c) -> p j c", j=J), kvg[:, r % R, :, 0:D],
                                      bank[2 + b][:, 0:J * D].rearrange("p (j c) -> p j c", j=J),
                                      ALU.mult).then_inc(s_p1, 1)

                def products_q(r):
                    b = r % 2
                    dve.wait_ge(s_p1, ready(i, r))
                    dve.tensor_tensor(prod[:, b, :], prod[:, b, :], bank[4 + b][:, 0:J * D],
                                      ALU.mult).then_inc(s_p2, 1)

                def head_sums(r):
                    b = r % 2
                    dve.wait_ge(s_p2, ready(i, r))
                    dve.wait_ge(s_exp, freed(i, r, 2))
                    dve.reduce_sum(sc[:, b, :], prod[:, b, :].rearrange("p (h d) -> p h d", d=HD),
                                   AX.X).then_inc(s_p3, 1)

                def clip(r):
                    b = r % 2
                    dve.wait_ge(s_p3, ready(i, r))
                    dve.tensor_scalar(sc[:, b, :], sc[:, b, :], 5.0, -5.0, ALU.min, ALU.max).then_inc(s_clip, 1)

                def message(r):
                    b = r % 2
                    dve.wait_ge(s_exp, ready(i, r))
                    dve.tensor_tensor(msg[:, b, :, 0:D].rearrange("p j (h d) -> p j h d", d=HD),
                                      kvg[:, r % R, :, D:2 * D].rearrange("p j (h d) -> p j h d", d=HD),
                                      msg[:, b, :, D:DMSG].unsqueeze(3).to_broadcast([P, J, H, HD]),
                                      ALU.mult).then_inc(s_msg, 1)

                def add_window(r):
                    dve.wait_ge(s_agg, ready(i, r))
                    dve.wait_ge(s_acc2, freed(i, r, 1))
                    base = dve.value_load(base_i[0:1, bass.ds(i * R + r, 1)], min_val=0, max_val=N - W)
                    a = acc[0:DMSG, 0, bass.ds(base, W)]
                    dve.tensor_tensor(a, a, bank[6 + r % 2][0:DMSG, 0:W], ALU.add).then_inc(s_acc2, 1)

                for r in steps:
                    if live(r - 2):
                        products_e(r - 2)
                    if live(r):
                        one_hot(i, r, 1, s_agg, s_S2)
                    if live(r - 2):
                        products_q(r - 2)
                    if live(r - 3):
                        message(r - 3)
                    if live(r - 2):
                        head_sums(r - 2)
                    if live(r - 4):
                        add_window(r - 4)
                    if live(r - 2):
                        clip(r - 2)

            pipeline(dve, turn2, 4)

            dve.wait_ge(s_wv_c, NT)
            step(dve.tensor_scalar_add(nrz[:, :, :], h_stage[:, :, D:DMSG], 1e-6))
            step(dve.reciprocal(nrz[:, :, :], nrz[:, :, :]))
            step(dve.tensor_tensor(qN[:, :, :].rearrange("p t (h d) -> p t h d", d=HD),
                                   h_stage[:, :, 0:D].rearrange("p t (h d) -> p t h d", d=HD),
                                   nrz[:, :, :].unsqueeze(3).to_broadcast([P, NT, H, HD]), ALU.mult))
            step(dve.tensor_tensor(xN[:, :, :], xN[:, :, :], qN[:, :, :], ALU.add))
            layer_norm(s_fin)

        @block.tensor
        def _(pe):
            for s in (s_hpT, s_keepP, s_sum, s_back, s_max, s_T, s_EQ, s_agg):
                pe.sem_inc(s, AHEAD)
            pe.wait_ge(s_iden, 6)
            pe.wait_ge(s_base, 1)
            pe.matmul(bank[7][:, 0:NG], first_row[:, :], tmpE[:, :, 0], start=True, stop=True).then_inc(s_baseP, 1)
            pe.wait_ge(s_x, 32)
            pe.wait_ge(s_wb, 160)
            pe.wait_ge(s_free0, 1)
            for i in range(NT // K7):
                for k in range(K7):
                    t = i * K7 + k
                    pe.transpose(bank[k][0:D, 0:P], xN[:, bass.ds(t, 1), :].rearrange("p a c -> p (a c)"),
                                 ident[:, :]).then_inc(s_xT_p, 1)
                for k in range(K7):
                    t = i * K7 + k
                    pe.wait_ge(s_xT_c, i * K7 + (k + 1))
                    pe.matmul(bank[k][:, 128:128 + D], xT[:, bass.ds(t * P, P)], w_pool[:, :],
                              start=True, stop=True).then_inc(s_hp_p, 1)
                pe.wait_ge(s_hp_c, i * K7 + K7)

            pe.wait_ge(s_rel, 1)
            def turn1(i, steps, live):
                def front(r):
                    b = r % 2
                    pe.wait_ge(s_gat[r], landed(i, r, 16 * J))
                    pe.wait_ge(s_scan, freed(i, r, 2))
                    for j in range(J):
                        last = pe.transpose(bank[b][0:D, j:GE:J], gat[:, r, j, DSUM:XROW], ident[:, :])
                    last.then_inc(s_hpT, 1)
                    pe.wait_ge(s_keepC, freed(i, r, 2))
                    for j in range(J):
                        last = pe.matmul(bank[2 + b][0:D, j:GE:J],
                                         keep[:, bass.ds(i * R + r, 1), j].to_broadcast([P, D]), identb[:, :],
                                         start=True, stop=True)
                    last.then_inc(s_keepP, 1)
                    pe.wait_ge(s_S, ready(i, r))
                    pe.wait_ge(s_acc, freed(i, r, 2))
                    for j in range(J):
                        last = pe.matmul(bank[6 + b][0:DSUM, 0:W], gat[:, r, j, 0:DSUM], S[:, r % R, j, :],
                                         start=j == 0, stop=j == J - 1)
                    last.then_inc(s_sum, 1)

                def back(r):
                    b = r % 2
                    pe.wait_ge(s_scan, ready(i, r))
                    pe.wait_ge(s_bcp, freed(i, r, 2))
                    for j in range(J):
                        last = pe.transpose(bank[4 + b][:, j * D:(j + 1) * D], scan[:, b, j:GE:J], ident[0:D, 0:D])
                    last.then_inc(s_back, 1)

                def ends(r):
                    b = r % 2
                    pe.wait_ge(s_bcp, ready(i, r))
                    for j in range(J):
                        last = pe.matmul(bank[6 + b][0:DSUM, W:2 * W], scanE[:, b, j, :], S[:, r % R, J + j, :],
                                         start=j == 0, stop=j == J - 1)
                    last.then_inc(s_max, 1)

                for r in steps:
                    if live(r - 2):
                        ends(r - 2)
                    if live(r):
                        front(r)
                    if live(r - 1):
                        back(r - 1)

            pipeline(pe, turn1, 2)

            pe.wait_ge(s_acc, NG + AHEAD)
            pe.wait_ge(s_w, 64)
            with pe.Fori(0, NP // CH) as i:
                at = bass.ds(i * CH, CH)
                pe.matmul(bank[0][0:D, 0:CH], last_row[:, :], acc[0:DSUM, 0, at],
                          start=True, stop=True).then_inc(s_deg, 1)
                pe.wait_ge(s_mean, i * 3 + 3)
                for m, (ws, wn, agg) in enumerate(((w_self1, w_neigh1, meanT[:, :]),
                                                   (w_self2, w_neigh2, acc[0:D, 1, at]))):
                    pe.matmul(bank[1 + m][0:D, 0:CH], ws[:, :], xT[0:D, at], start=True, stop=False)
                    last = pe.matmul(bank[1 + m][0:D, 0:CH], wn[:, :], agg, start=False, stop=True)
                last.then_inc(s_lin, 1)
                pe.wait_ge(s_linc, i + 1)

            pe.wait_ge(s_hT, 1)
            for i in range(NT // K7):
                for k in range(K7):
                    pe.transpose(bank[k][:, 0:D], acc[0:D, 0, bass.ds((i * K7 + k) * P, P)],
                                 ident[0:D, 0:D]).then_inc(s_hN_p, 1)
                pe.wait_ge(s_hN_c, i * K7 + K7)

            pe.wait_ge(s_x1, 1)
            for i in range(NT // K7):
                for k in range(K7):
                    pe.transpose(bank[k][0:D, 0:P], xN[:, bass.ds(i * K7 + k, 1), :].rearrange("p a c -> p (a c)"),
                                 ident[:, :]).then_inc(s_x1_p, 1)
                for k in range(K7):
                    at = bass.ds((i * K7 + k) * P, P)
                    pe.wait_ge(s_x1_c, i * K7 + (k + 1))
                    pe.matmul(bank[k][:, 128:128 + 2 * D], xT[:, at], w_kv[:, :], start=True, stop=True)
                    pe.matmul(bank[k][:, 320:320 + D], xT[:, at], w_q[:, :], start=True,
                              stop=True).then_inc(s_kv_p, 1)
                pe.wait_ge(s_kv_c, i * K7 + K7)
                pe.wait_ge(s_q_c, i * K7 + K7)

            def turn2(i, steps, live):
                def transposes(r):
                    b = r % 2
                    pe.wait_ge(s_ea[r], i * 16 + 16)
                    pe.wait_ge(s_tc, freed(i, r, 1))
                    pe.wait_ge(s_S2, ready(i, r))
                    for j in range(J):
                        pe.transpose(bank[0][0:D, j * P:(j + 1) * P], ea[:, r, j, :], ident[:, :])
                    for j in range(J):
                        last = pe.transpose(bank[1][0:W, j * P:(j + 1) * P], S[:, r % R, j, :], ident[:, :])
                    last.then_inc(s_T, 1)

                def expand(r):
                    b = r % 2
                    pe.wait_ge(s_tc, ready(i, r))
                    pe.wait_ge(s_qw[r % R], landed(i, r, 16))
                    pe.wait_ge(s_p2, freed(i, r, 2))
                    for j in range(J):
                        pe.matmul(bank[2 + b][:, j * D:(j + 1) * D], eaC[:, b, j * P:(j + 1) * P], w_e[:, :],
                                  start=True, stop=True)
                    for j in range(J):
                        last = pe.matmul(bank[4 + b][:, j * D:(j + 1) * D], stC[:, b, j * P:(j + 1) * P],
                                         qwin[:, r % R, :], start=True, stop=True)
                    last.then_inc(s_EQ, 1)

                def aggregate(r):
                    b = r % 2
                    pe.wait_ge(s_msg, ready(i, r))
                    pe.wait_ge(s_acc2, freed(i, r, 2))
                    for j in range(J):
                        last = pe.matmul(bank[6 + b][0:DMSG, 0:W], msg[:, b, j, :], S[:, r % R, j, :],
                                         start=j == 0, stop=j == J - 1)
                    last.then_inc(s_agg, 1)

                for r in steps:
                    if live(r - 1):
                        expand(r - 1)
                    if live(r):
                        transposes(r)
                    if live(r - 3):
                        aggregate(r - 3)

            pipeline(pe, turn2, 3)

            pe.wait_ge(s_acc2, NG + AHEAD)
            for i in range(NT // K7):
                for k in range(K7):
                    pe.transpose(bank[k][:, 0:DMSG], acc[0:DMSG, 0, bass.ds((i * K7 + k) * P, P)],
                                 ident[0:DMSG, 0:DMSG]).then_inc(s_wv_p, 1)
                pe.wait_ge(s_wv_c, i * K7 + K7)


_WEIGHTS = ['L0_gnn_W_self1', 'L0_gnn_W_neigh1', 'L0_gnn_W_pool', 'L0_gnn_b_pool', 'L0_gnn_W_self2', 'L0_gnn_W_neigh2',
            'L0_gnn_g1', 'L0_gnn_beta1', 'L0_gnn_g2', 'L0_gnn_beta2', 'L1_gnn_Wq', 'L1_gnn_bq', 'L1_gnn_Wk',
            'L1_gnn_bk', 'L1_gnn_We', 'L1_gnn_be', 'L1_gnn_Wv', 'L1_gnn_bv']


def kernel(**inputs):
    import numpy as _np
    import concourse.bacc as _bacc
    from concourse import mybir as _mybir
    from concourse.bass_utils import run_bass_kernel_spmd as _run

    def split(a):
        whole = a[:FULL * GE].reshape(FULL, P, J).transpose(1, 0, 2).reshape(P, FULL * J)
        return _np.ascontiguousarray(whole), _np.ascontiguousarray(a[FULL * GE:])

    src, dst = _np.asarray(inputs['src']), _np.asarray(inputs['dst'])
    named = [('x', inputs['x'])]
    for name, a in (('src', src), ('dst', dst), ('before', _np.concatenate([dst[:1], dst[:-1]])), ('after', dst[1:])):
        whole, rest = split(a)
        named += [(name + '_groups', whole), (name + '_rest', rest)]
    named += [('edge_attr', inputs['edge_attr_96'])] + [(n, inputs[n]) for n in _WEIGHTS]
    nc = _bacc.Bacc("TRN2", target_bir_lowering=False, num_devices=1)
    arrays, args = {}, []
    for name, a in named:
        a = _np.ascontiguousarray(a)
        arrays[f"in_{name}_dram"] = a
        args.append(nc.dram_tensor(f"in_{name}_dram", a.shape, _mybir.dt.from_np(a.dtype), kind="ExternalInput").ap())
    args.append(nc.dram_tensor("out_0_dram", (N, D), _mybir.dt.float32, kind="ExternalOutput").ap())
    build(nc, *args)
    return _run(nc, [arrays], core_ids=[0]).results[0]["out_0_dram"]
```

```python
import concourse.bass as bass
from concourse import mybir
from contextlib import ExitStack

F32 = mybir.dt.float32
BF16 = mybir.dt.bfloat16
I32 = mybir.dt.int32
ALU = mybir.AluOpType
ACT = mybir.ActivationFunctionType
AX = mybir.AxisListType

N, D, E = 6250, 96, 206250
H = 8
HD = D // H
P = 128
J = 4
GE = P * J
FULL = E // GE
TAIL = E - FULL * GE
R = 4
TURNS = -(-(FULL + 1) // R)
NG = TURNS * R
W = 64
NT = -(-N // P)
NFULL = N // P
NTAIL = N - NFULL * P
NP = NT * P
K7 = 7
KC = K7 * P
NK = NT // K7
NCH = 14
CH = NP // NCH
LAST = N - (NCH - 1) * CH
TRANS = 3
XTURNS = 1 + -(-NT // (TRANS * R))
HALVES = ((0, 4), (4, K7))
KV_BANKS = (6, 7, 4, 5)
DSUM = D + 1
DMSG = D + H
PAD_DST = -1
EC = 125
NEC = E // EC
EPS = 1e-5
AHEAD = 4


def build(nc, x, src, dst, src_m, src_t, dst_m, dst_t, prv_m, prv_t, nxt_m, nxt_t, edge_attr, Ws1, Wn1, Wp, bp, Ws2, Wn2,
          g1, be1, g2, be2, Wq, bq, Wk, bk, We, be, Wv, bv, out):
    ctx = ExitStack()
    with ctx:
        def sb(name, shape, dt=F32):
            return ctx.enter_context(nc.sbuf_tensor(name, shape, dt))

        def sem(name):
            return ctx.enter_context(nc.semaphore(name))

        counts_row = nc.dram_tensor("counts_row", (NP,), F32, kind="Internal").ap()
        kv_table = nc.dram_tensor("kv_table", (NP, 2 * D), F32, kind="Internal").ap()

        xN = sb("xN", [P, NT, D])
        stage = sb("stage", [P, NT, 2 * D])
        xT = sb("xT", [DSUM, NP])
        acc = sb("acc", [P, 2, NP])
        flat = stage[:, :, :].rearrange("p t c -> p (t c)")
        spare, nxt, dsts, prv, tmpE = (flat[:, n * NG * J:(n + 1) * NG * J] for n in range(5))
        nxt_i, dst_i, prv_i = nxt.bitcast(I32), dsts.bitcast(I32), prv.bitcast(I32)
        spare, tmpE = spare.rearrange("p (g j) -> p g j", j=J), tmpE.rearrange("p (g j) -> p g j", j=J)

        src_all = sb("src_all", [P, (NG + R) * J], I32)
        rel = sb("rel", [P, NG, 2, J])
        keep = sb("keep", [P, NG, J], BF16)
        base_i = sb("base_i", [1, NG], I32)
        idx = sb("idx", [P, R, J], I32)

        kvg = sb("kvg", [P, R, J, 2 * D])
        xg = kvg[:, :, :, 0:DSUM]
        S = sb("S", [P, R, 2 * J, W])
        baseB = S[:, 0, :, :].rearrange("p j w -> p (j w)")[:, 0:NG]
        keepC = sb("keepC", [D, 2, GE], BF16)
        scan = sb("scan", [D, 2, GE])
        scanE = sb("scanE", [P, 2, J, D])
        ea = sb("ea", [P, R, J, D])
        xwin = sb("xwin", [DSUM, 2, W])
        qwin = sb("qwin", [W, 2, D])
        eaC = sb("eaC", [DSUM, 2, GE])
        xeC = eaC
        stC = scan[0:W, :, :]
        prod = sb("prod", [P, 2, J * D])
        sc = sb("sc", [P, 2, J * H])
        msg = sb("msg", [P, 2, J, DMSG])

        ident = sb("ident", [P, P])
        identb = sb("identb", [P, P], BF16)
        first_row = sb("first_row", [P, P])
        iotaW = sb("iotaW", [P, W])
        w_self1 = sb("w_self1", [D, D])
        w_neigh1 = sb("w_neigh1", [D, D])
        w_self2 = sb("w_self2", [D, D])
        w_neigh2 = sb("w_neigh2", [D, D])
        w_pool = sb("w_pool", [DSUM, D])
        w_kv = sb("w_kv", [DSUM, 2 * D])
        w_q = sb("w_q", [DSUM, D])
        w_e = sb("w_e", [DSUM, D])
        gb = sb("gb", [D, 4])
        eps_col = sb("eps_col", [P, 2])
        ones_col = sb("ones_col", [P, 1])
        warm = sb("warm", [1, 1])
        stats = sb("stats", [D, 2, NCH, 6])
        mv = sb("mv", [D, 2, 2])
        std = sb("std", [D, 2])
        rstd = sb("rstd", [D, 2])
        ga = sb("ga", [D, 2])
        sh = sb("sh", [D, 2])
        shs = sb("shs", [D, 1])
        small = keep[:, :, :].rearrange("p g j -> p (g j)").bitcast(F32)
        lnst = small[:, 0:K7 * 6].rearrange("p (k c) -> p k c", k=K7)
        lnmv = small[:, 64:64 + K7 * 2].rearrange("p (k c) -> p k c", k=K7)
        lnr = small[:, 192:192 + K7]
        lnb = small[:, 256:256 + K7]
        nz = small[:, 320:320 + K7 * H].rearrange("p (k h) -> p k h", k=K7)
        counts = small[:, 64:64 + NT]
        countsB = flat[0:D, 0:NP]
        hn = prod[:, :, :].rearrange("p b c -> p (b c)")[:, 0:K7 * D].rearrange("p (k c) -> p k c", k=K7)

        bad = sb("bad", [P, 2])
        flag_i = sb("flag_i", [1, 1], I32)
        ends_i = prod[0:1, 1, 0:2 * EC].rearrange("p (a c) -> p a c", a=2).bitcast(I32)
        hpT = flat[0:D, 0:NP]
        kT, qT, vT = flat[0:D, 0:NP], acc[0:D, 1, :], xT[0:D, :]
        kq = prod[0:D, 0, 0:EC]
        msgs = msg[0:DMSG, :, :, :].rearrange("p b j c -> p (b j c)")
        vE, weight, weighted = msgs[:, 0:EC], msgs[:, EC:2 * EC], msgs[:, 2 * EC:3 * EC]
        same_head = kvg[0:D, 0, :, :].rearrange("p j c -> p (j c)")[:, 0:DMSG]

        bank = [ctx.enter_context(nc.psum_tensor(f"bank{k}", [P, 512], F32)) for k in range(8)]

        s_x = [sem(f"s_x_part{k}") for k in range(NK)]
        s_w, s_wp, s_wb, s_gb = sem("s_w"), sem("s_wp"), sem("s_wb"), sem("s_gb")
        s_src, s_dst, s_prv, s_nxt = sem("s_src"), sem("s_dst"), sem("s_prv"), sem("s_nxt")
        s_kvtab, s_out = sem("s_kvtab"), sem("s_out")
        s_gat = [sem(f"s_gat{r}") for r in range(R)]
        s_kvg = [sem(f"s_kvg{r}") for r in range(R)]
        s_ea = [sem(f"s_ea{r}") for r in range(R)]
        s_tail = sem("s_tail")
        s_zero, s_pads, s_iden = sem("s_zero"), sem("s_pads"), sem("s_iden")
        s_v = sem("s_v")
        s_base, s_baseP, s_rel = sem("s_base"), sem("s_baseP"), sem("s_rel")
        s_ones = sem("s_ones")
        s_idx, s_free0, s_S, s_xe, s_xec, s_hpT = (sem("s_idx"), sem("s_free0"), sem("s_S"), sem("s_xe"),
                                                   sem("s_xec"), sem("s_hpT"))
        s_sum, s_scan, s_back, s_bcp, s_max, s_acc, s_accm = (sem("s_sum"), sem("s_scan"), sem("s_back"),
                                                              sem("s_bcp"), sem("s_max"), sem("s_acc"),
                                                              sem("s_accm"))
        s_deg, s_mean, s_lin, s_linc, s_bn, s_std = (sem("s_deg"), sem("s_mean"), sem("s_lin"), sem("s_linc"),
                                                     sem("s_bn"), sem("s_std"))
        s_stat, s_u, s_z, s_hN, s_lst, s_mv, s_sd, s_rs, s_nb, s_x1 = (
            sem("s_stat"), sem("s_u"), sem("s_z"), sem("s_hN"), sem("s_lst"), sem("s_mv"), sem("s_sd"), sem("s_rs"),
            sem("s_nb"), sem("s_x1"))
        s_h, s_row = sem("s_h"), sem("s_row")
        s_x1T, s_x1c, s_kv, s_kvD, s_kvA = sem("s_x1T"), sem("s_x1c"), sem("s_kv"), sem("s_kvD"), sem("s_kvA")
        s_idx2, s_S2, s_T, s_tc, s_EQ = sem("s_idx2"), sem("s_S2"), sem("s_T"), sem("s_tc"), sem("s_EQ")
        s_p1, s_p2, s_p3, s_clip, s_exp = sem("s_p1"), sem("s_p2"), sem("s_p3"), sem("s_clip"), sem("s_exp")
        s_msg, s_agg, s_acc2 = sem("s_msg"), sem("s_agg"), sem("s_acc2")
        s_Te, s_ec = sem("s_Te"), sem("s_ec")
        s_xw, s_q, s_qc = sem("s_xw"), sem("s_q"), sem("s_qc")
        s_bad, s_flag, s_flag_c = sem("s_bad"), sem("s_flag"), sem("s_flag_c")
        s_ends, s_used, s_edge, s_made0 = sem("s_ends"), sem("s_used"), sem("s_edge"), sem("s_made0")
        s_hp, s_hpc = sem("s_hp"), sem("s_hpc")
        s_ends2, s_used2, s_edge2, s_made1, s_kqv, s_kqvc, s_mask = (
            sem("s_ends2"), sem("s_used2"), sem("s_edge2"), sem("s_made1"), sem("s_kqv"), sem("s_kqvc"),
            sem("s_mask"))
        s_eaT, s_eaTc, s_eE, s_kq, s_kqe, s_dot, s_dotc, s_w2, s_wd = (
            sem("s_eaT"), sem("s_eaTc"), sem("s_eE"), sem("s_kq"), sem("s_kqe"), sem("s_dot"), sem("s_dotc"),
            sem("s_w2"), sem("s_wd"))
        s_tick = sem("s_tick")
        s_wv, s_nz, s_hn, s_add, s_lst2, s_mv2, s_sd2, s_rs2, s_nb2, s_fin = (
            sem("s_wv"), sem("s_nz"), sem("s_hn"), sem("s_add"), sem("s_lst2"), sem("s_mv2"), sem("s_sd2"),
            sem("s_rs2"), sem("s_nb2"), sem("s_fin"))

        def ready(i, r):
            return i * R + (r + 1 + AHEAD)

        def freed(i, r, depth):
            return i * R + (r + 1 + AHEAD - depth)

        def landed(i, r, per_turn):
            return (i + r // R) * per_turn + per_turn

        def wait_past(eng, s, value):
            if not (isinstance(value, int) and value <= 0):
                eng.wait_ge(s, value)

        def pipeline(eng, turn, lag, turns=TURNS, per=R, peel=0, between=()):
            peel = max(peel, -(-lag // per))
            for p in range(peel):
                turn(p, range(per), lambda r: p * per + r >= 0)
                for work in between[p:p + 1]:
                    work()
            if peel < turns:
                with eng.Fori(peel, turns) as i:
                    turn(i, range(per), lambda r: True)
            turn(turns, range(lag), lambda r: r < 0)

        def node_rows(t, k):
            return bank[t % 2 * 2 + k // 4][:, (k % 4) * D:(k % 4 + 1) * D]

        def own_tiles(i, r):
            g = (i - 1) * R + r if isinstance(i, int) else NT
            return range(0) if g < 0 else range(min(g * TRANS, NT), min((g + 1) * TRANS, NT))

        def irregular(eng):
            eng.wait_ge(s_flag_c, 1)
            flag = eng.value_load(flag_i[0:1, 0:1], min_val=0, max_val=2 * E)
            return eng.If(flag > 0)

        block = ctx.enter_context(nc.Block())

        @block.sync
        def _(sp):
            def edges(to, main, tail, done):
                n = tail.shape[0]
                sp.dma_start(to[:, 0:FULL * J], main).then_inc(done, 16)
                sp.dma_start(to[0:n // J, FULL * J:(FULL + 1) * J],
                             tail[0:n // J * J].rearrange("(p j) -> p j", j=J)).then_inc(done, 16)
                sp.dma_start(to[n // J:n // J + 1, FULL * J:FULL * J + n % J],
                             tail[n // J * J:n].rearrange("(a j) -> a j", a=1)).then_inc(done, 16)

            sp.wait_ge(s_pads, 1)
            edges(src_all, src_m, src_t, s_src)
            sp.wait_ge(s_pads, 2)
            edges(dst_i, dst_m, dst_t, s_dst)
            sp.dma_start(w_pool[0:D, :], Wp[:, :]).then_inc(s_wp, 16)
            sp.dma_start(w_pool[D:DSUM, :], bp.rearrange("(a c) -> a c", a=1)).then_inc(s_wp, 16)
            sp.wait_ge(s_pads, 3)
            edges(prv_i, prv_m, prv_t, s_prv)
            sp.wait_ge(s_pads, 4)
            edges(nxt_i, nxt_m, nxt_t, s_nxt)
            sp.wait_ge(s_zero, 1)
            for i in range(NK):
                sp.wait_ge(s_xe, ready(0, 2 * i))
                tiles = min(K7, NFULL - i * K7)
                sp.dma_start(xN[:, i * K7:i * K7 + tiles, :],
                             x[i * KC:i * KC + tiles * P, :].rearrange("(t p) c -> p t c", p=P)).then_inc(s_x[i], 16)
            sp.dma_start(xN[0:NTAIL, NFULL, :], x[NFULL * P:N, :]).then_inc(s_x[NK - 1], 16)
            for w, v in ((w_self1, Ws1), (w_neigh1, Wn1), (w_self2, Ws2), (w_neigh2, Wn2)):
                sp.dma_start(w[:, :], v[:, :]).then_inc(s_w, 16)
            for w, v, b in ((w_kv[:, 0:D], Wk, bk), (w_kv[:, D:2 * D], Wv, bv),
                            (w_q[:, :], Wq, bq), (w_e[:, :], We, be)):
                sp.dma_start(w[0:D, :], v[:, :]).then_inc(s_wb, 16)
                sp.dma_start(w[D:D + 1, :], b.rearrange("(a c) -> a c", a=1)).then_inc(s_wb, 16)
            with nc.allow_non_contiguous_dma(reason="four columns of 96 numbers"):
                for n, v in enumerate((g1, be1, g2, be2)):
                    sp.dma_start(gb[:, n:n + 1], v.rearrange("(c a) -> c a", a=1)).then_inc(s_gb, 16)

            def load_ends(c, done):
                for n, a in enumerate((src, dst)):
                    sp.dma_start(ends_i[:, n, :], a[bass.ds(c * EC, EC)].rearrange("(a c) -> a c", a=1)
                                 ).then_inc(done, 16)

            with irregular(sp):
                with sp.Fori(0, NEC) as c:
                    sp.wait_ge(s_used, c + 1)
                    load_ends(c, s_ends)

            sp.wait_ge(s_deg, 1)
            sp.dma_start(counts, acc[D:DSUM, 0, :].rearrange("a (p t) -> a p t", t=NT)).then_inc(s_row, 16)
            sp.wait_ge(s_deg, 2)
            sp.dma_start(counts_row.rearrange("(p t) -> p t", t=NT), counts).then_inc(s_row, 16)
            sp.wait_ge(s_row, 32)
            sp.dma_start(countsB, counts_row.rearrange("(a n) -> a n", a=1).to_broadcast([D, NP])
                         ).then_inc(s_row, 16)

            ea_v = edge_attr[0:FULL * GE, :].rearrange("(g p j) c -> p g (j c)", p=P, j=J)

            def load_group(i, r):
                sp.dma_start(ea[:, r, :, :].rearrange("p j c -> p (j c)"),
                             ea_v[:, bass.ds(i * R + r, 1), :].rearrange("p g c -> p (g c)")).then_inc(s_ea[r], 16)

            for r in range(R):
                load_group(0, r)

            def store_table(i, k0, k1):
                sp.dma_start(kv_table[bass.ds(i * KC + k0 * P, (k1 - k0) * P), :].rearrange("(t p) c -> p t c", p=P),
                             stage[:, bass.ds(i * K7 + k0, k1 - k0), :]).then_inc(s_kvtab, 16)

            with sp.Fori(0, NK - 1) as i:
                sp.wait_ge(s_kvD, i * 2 + 2)
                sp.wait_ge(s_kvA, i * 2 + 2)
                store_table(i, 0, K7)
            for n, (k0, k1) in enumerate(HALVES):
                sp.wait_ge(s_kvD, (NK - 1) * 2 + n + 1)
                sp.wait_ge(s_kvA, (NK - 1) * 2 + n + 1)
                store_table(NK - 1, k0, k1)

            with sp.Fori(1, FULL // R) as i:
                for r in range(R):
                    sp.wait_ge(s_T, freed(i, r, R))
                    load_group(i, r)

            def tail_load(g, r):
                if g < FULL:
                    sp.dma_start(ea[:, r, :, :].rearrange("p j c -> p (j c)"), ea_v[:, g, :]).then_inc(s_ea[r], 16)
                elif g == FULL:
                    e0, whole = FULL * GE, TAIL // J
                    sp.dma_start(ea[0:whole, r, :, :].rearrange("p j c -> p (j c)"),
                                 edge_attr[e0:e0 + whole * J, :].rearrange("(p j) c -> p (j c)", j=J)
                                 ).then_inc(s_tail, 16)
                    sp.wait_ge(s_tail, 16)
                    sp.dma_start(ea[whole:whole + 1, r, 0:TAIL % J, :].rearrange("p j c -> p (j c)"),
                                 edge_attr[e0 + whole * J:E, :].rearrange("(a j) c -> a (j c)", a=1)
                                 ).then_inc(s_ea[r], 16)
                else:
                    sp.sem_inc(s_ea[r], 16)

            for g in range(FULL // R * R, NG):
                sp.wait_ge(s_T, freed(g // R, g % R, R))
                tail_load(g, g % R)

            with irregular(sp):
                with sp.Fori(0, NEC) as c:
                    sp.wait_ge(s_used2, c + 1)
                    load_ends(c, s_ends2)
                    sp.dma_start(ea[0:EC, 0, 0, :], edge_attr[bass.ds(c * EC, EC), :]).then_inc(s_ends2, 16)

            def store(i, tiles):
                sp.wait_ge(s_fin, i * K7 + K7)
                sp.dma_start(out[bass.ds(i * KC, tiles * P), :].rearrange("(t p) c -> p t c", p=P),
                             xN[:, bass.ds(i * K7, tiles), :]).then_inc(s_out, 16)

            with sp.Fori(0, NK - 1) as i:
                store(i, K7)
            store(NK - 1, K7 - 1)
            sp.dma_start(out[NFULL * P:N, :], xN[0:NTAIL, NFULL, :]).then_inc(s_out, 16)
            sp.wait_ge(s_out, 16 * (NK + 1))

        @block.gpsimd
        def _(pool):
            pool.memset(xN[:, NFULL, :], 0.0).then_inc(s_zero, 1)
            pool.memset(ident[:, :], 0.0).then_inc(s_iden, 1)
            pool.memset(first_row[:, :], 1.0).then_inc(s_iden, 1)
            pool.iota(iotaW[:, :], pattern=[[1, W]], base=0, channel_multiplier=0,
                      allow_small_or_imprecise_dtypes=True).then_inc(s_iden, 1)
            pool.wait_ge(s_iden, 3)
            pool.affine_select(out=ident[:, :], in_=ident[:, :], compare_op=ALU.not_equal, fill=1.0, base=0,
                               pattern=[[-1, P]], channel_multiplier=1).then_inc(s_iden, 1)
            pool.affine_select(out=first_row[:, :], in_=first_row[:, :], compare_op=ALU.is_equal, fill=0.0, base=0,
                               pattern=[[0, P]], channel_multiplier=1).then_inc(s_iden, 1)
            pool.wait_ge(s_iden, 5)
            pool.tensor_copy(identb[:, :], ident[:, :]).then_inc(s_iden, 1)

            def gathers(table, to, s_i, s_free, s_done):
                def gather(i, r):
                    pool.wait_ge(s_i, ready(i, r))
                    pool.sem_inc(s_tick, 1)
                    pool.wait_ge(s_free, freed(i, r, R))
                    pool.sem_inc(s_tick, 1)
                    some = 1 if isinstance(i, int) and i * R + r > FULL else J
                    for j in range(some):
                        pool.indirect_dma_start(
                            out=to[:, r, j, :], out_offset=None, in_=table,
                            in_offset=bass.IndirectOffsetOnAxis(ap=idx[:, r, j:j + 1], axis=0)
                        ).then_inc(s_done[r], 16 * J // some)

                with pool.Fori(0, TURNS - 1) as i:
                    for r in range(R):
                        gather(i, r)
                for r in range(R):
                    gather(TURNS - 1, r)

            pool.wait_ge(s_ones, 1)
            gathers(x, kvg[:, :, :, 0:D], s_idx, s_sum, s_gat)
            with pool.Fori(0, NK) as i:
                at = bass.ds(i * KC, KC)
                pool.wait_ge(s_z, i * 2 + 3)
                pool.sem_inc(s_tick, 1)
                pool.tensor_tensor(acc[0:D, 0, at], acc[0:D, 1, at], xT[0:D, at], ALU.add).then_inc(s_h, 1)
            pool.wait_ge(s_hN, NK)
            pool.memset(acc[:, 0, :], 0.0).then_inc(s_free0, 1)
            pool.wait_ge(s_kvtab, 16 * (NK + 1))
            gathers(kv_table, kvg, s_idx2, s_msg, s_kvg)

            def last_residual():
                k0, k1 = HALVES[1]
                with pool.Fori(0, NK) as i:
                    own = bass.ds(i * K7 + k0, k1 - k0)
                    pool.wait_ge(s_hn, i * 2 + 2)
                    pool.sem_inc(s_tick, 1)
                    pool.tensor_tensor(xN[:, own, :], xN[:, own, :], hn[:, k0:k1, :], ALU.add).then_inc(s_add, 1)

            with irregular(pool):
                pool.wait_ge(s_msg, NG + AHEAD)
                pool.memset(same_head, 1.0).then_inc(s_mask, 1)
                pool.wait_ge(s_mask, 1)
                done = 1
                for base, sign in ((0, 1), (HD - 1, -1)):
                    for view, inner in ((same_head[:, 0:D].rearrange("p (h d) -> p h d", d=HD), [[0, HD]]),
                                        (same_head[:, D:DMSG], [])):
                        pool.affine_select(out=view, in_=view, compare_op=ALU.is_ge, fill=0.0, base=base,
                                           pattern=[[-sign * HD, H]] + inner, channel_multiplier=sign
                                           ).then_inc(s_mask, 1)
                        done += 1
                        pool.wait_ge(s_mask, done)
            last_residual()

        def copy_indices(act, i, r, s_done, s_i):
            act.wait_ge(s_done[r % R], landed(i, r, 16 * J))
            act.copy(idx[:, r % R, :], src_all[:, bass.ds((i * R + (r + R)) * J, J)]).then_inc(s_i, 1)

        @block.scalar
        def _(act):
            for s in (s_xec, s_bcp, s_xw, s_ec, s_tc, s_exp):
                act.sem_inc(s, AHEAD)
            act.wait_ge(s_ones, 2)
            act.copy(warm[:, :], ones_col[0:1, :])
            act.wait_ge(s_src, 48)
            act.copy(idx[:, :, :].rearrange("p r j -> p (r j)"), src_all[:, 0:R * J]).then_inc(s_idx, R + AHEAD)
            act.copy(acc[:, 1, :], eps_col[:, 1:2].to_broadcast([P, NP])).then_inc(s_free0, 1)
            act.copy(xT[D:DSUM, :], ones_col[D:DSUM, :].to_broadcast([1, NP]))
            act.copy(eaC[D:DSUM, :, :].rearrange("p b e -> p (b e)"), ones_col[D:DSUM, :].to_broadcast([1, 2 * GE]))

            def turn1(i, steps, live):
                def front_copy(r):
                    copy_indices(act, i, r, s_gat, s_idx)
                    act.wait_ge(s_xe, ready(i, r))
                    act.wait_ge(s_scan, freed(i, r, 2))
                    act.copy(xeC[0:D, r % 2, :], bank[0][0:D, :])
                    act.copy(keepC[:, r % 2, :], bank[1][0:D, :]).then_inc(s_xec, 1)

                def back_copy(r):
                    act.wait_ge(s_back, ready(i, r))
                    act.wait_ge(s_max, freed(i, r, 2))
                    act.copy(scanE[:, r % 2, :, :],
                             bank[4 + r % 2][:, 0:J * D].rearrange("p (j c) -> p j c", j=J)).then_inc(s_bcp, 1)

                for r in steps:
                    if live(r):
                        front_copy(r)
                    if live(r - 2):
                        back_copy(r - 2)

            pipeline(act, turn1, 2)

            def linear(m, first):
                def chunk(i, steps, live):
                    for r in steps:
                        c = i * 2 + r
                        act.wait_ge(s_lin, c + (first + 1))
                        act.copy(acc[0:D, m, bass.ds(c * CH, CH)], bank[r % 2][0:D, 0:CH]).then_inc(s_linc, 1)
                return chunk

            pipeline(act, linear(1, 0), 0, NCH // 2, 2)
            pipeline(act, linear(0, NCH), 0, NCH // 2, 2)
            act.wait_ge(s_bn, 1)
            act.activation(std[:, :], mv[:, :, 1], ACT.Sqrt, bias=eps_col[0:D, 0:1]).then_inc(s_std, 1)
            act.wait_ge(s_z, 1)

            def nodes(i, steps, live):
                def branch2(t):
                    o2 = acc[0:D, 1, bass.ds(t * KC, KC)]
                    act.activation(o2, o2, ACT.Identity, bias=shs[:, :], scale=ga[:, 1:2]).then_inc(s_u, 1)

                def transposed(t):
                    act.wait_ge(s_x1T, t + 1)
                    for h, (k0, k1) in enumerate(HALVES):
                        last = act.copy(xT[0:D, bass.ds(t * KC + k0 * P, (k1 - k0) * P)],
                                        bank[4 + h][0:D, 0:(k1 - k0) * P])
                    last.then_inc(s_x1c, 1)

                def copies(t):
                    for n, tiles in ((1, 2), (3, 1)):
                        act.wait_ge(s_kv, t * 4 + (n + 1))
                        act.copy(stage[:, bass.ds(t * K7 + 2 * n, tiles), :].rearrange("p a c -> p (a c)"),
                                 bank[KV_BANKS[n]][:, 0:tiles * 2 * D]).then_inc(s_kvA, 1)

                def normalize(t):
                    act.wait_ge(s_mv, t + 1)
                    act.activation(lnr[:, :], lnmv[:, :, 1:2].rearrange("p t a -> p (t a)"), ACT.Sqrt,
                                   bias=eps_col[:, 0:1]).then_inc(s_sd, 1)
                    act.wait_ge(s_nb, t + 1)
                    for k in range(K7):
                        last = act.activation(xN[:, bass.ds(t * K7 + k, 1), :].rearrange("p a c -> p (a c)"),
                                              node_rows(t, k), ACT.Identity,
                                              bias=lnb[:, k:k + 1], scale=lnr[:, k:k + 1])
                    last.then_inc(s_x1, 1)

                for r in steps:
                    if live(r):
                        branch2(i + r)
                    if live(r - 3):
                        transposed(i + (r - 3))
                    if live(r - 2):
                        normalize(i + (r - 2))
                    if live(r - 3):
                        copies(i + (r - 3))

            pipeline(act, nodes, 3, NK, 1, peel=NK)
            act.copy(idx[:, :, :].rearrange("p r j -> p (r j)"), src_all[:, 0:R * J]).then_inc(s_idx2, R + AHEAD)

            def turn2(i, steps, live):
                def window(r):
                    base = act.value_load(base_i[0:1, bass.ds(i * R + r, 1)], min_val=0, max_val=N - W)
                    act.wait_ge(s_q, freed(i, r, 2))
                    act.copy(xwin[:, r % 2, :], xT[:, bass.ds(base, W)]).then_inc(s_xw, 1)

                def T_copy(r):
                    act.wait_ge(s_Te, ready(i, r))
                    act.wait_ge(s_EQ, freed(i, r, 2))
                    act.copy(eaC[0:D, r % 2, :], bank[0][0:D, :]).then_inc(s_ec, 1)
                    act.wait_ge(s_T, ready(i, r))
                    act.copy(stC[:, r % 2, :], bank[1][0:W, :]).then_inc(s_tc, 1)

                def exp(r):
                    act.wait_ge(s_clip, ready(i, r))
                    act.wait_ge(s_agg, freed(i, r, 2))
                    act.activation(msg[:, r % 2, :, D:DMSG], sc[:, r % 2, :].rearrange("p (j h) -> p j h", j=J),
                                   ACT.Exp).then_inc(s_exp, 1)

                for r in steps:
                    if live(r):
                        window(r)
                        T_copy(r)
                    if live(r - 2):
                        copy_indices(act, i, r - 2, s_kvg, s_idx2)
                        exp(r - 2)

            pipeline(act, turn2, 2)

            with irregular(act):
                with act.Fori(0, NEC) as c:
                    act.wait_ge(s_eaT, c + 1)
                    act.copy(eaC[0:D, 0, 0:EC], bank[0][0:D, 0:EC]).then_inc(s_eaTc, 1)
                    act.wait_ge(s_dotc, c + 1)
                    act.activation(weight, weight, ACT.Exp).then_inc(s_w2, 1)

            def last_norm(i, steps, live):
                if live(-1):
                    t0 = i - 1
                    act.wait_ge(s_nb2, t0 + 1)
                    for k in range(K7):
                        t = t0 * K7 + k
                        row = xN[:, bass.ds(t, 1), :].rearrange("p a c -> p (a c)")
                        act.activation(row, row, ACT.Identity, bias=lnb[:, k:k + 1],
                                       scale=lnr[:, k:k + 1]).then_inc(s_fin, 1)
                if live(0):
                    wait_past(act, s_fin, i * K7)
                    act.wait_ge(s_mv2, i + 1)
                    act.activation(lnr[:, :],
                                   lnmv[:, :, 1:2].rearrange("p t a -> p (t a)"), ACT.Sqrt,
                                   bias=eps_col[:, 0:1]).then_inc(s_sd2, 1)

            pipeline(act, last_norm, 1, NK, 1)

        @block.vector
        def _(dve):
            steps = [0]

            def step(ins):
                steps[0] += 1
                ins.then_inc(s_v, 1)
                dve.wait_ge(s_v, steps[0])

            for s in (s_S, s_scan, s_acc, s_accm, s_S2, s_p1, s_p2, s_p3, s_clip, s_msg, s_acc2, s_qc):
                dve.sem_inc(s, AHEAD)
            pad = FULL * J
            dve.memset(src_all[:, pad:], 0).then_inc(s_pads, 1)
            dve.memset(dst_i[:, pad:], PAD_DST).then_inc(s_pads, 1)
            dve.memset(prv_i[:, pad:], PAD_DST - 1).then_inc(s_pads, 1)
            dve.memset(nxt_i[:, pad:], PAD_DST - 1).then_inc(s_pads, 1)
            dve.memset(kvg[:, :, :, D:DSUM], 1.0).then_inc(s_ones, 1)
            dve.memset(eps_col[:, 0:1], EPS)
            dve.memset(eps_col[:, 1:2], 0.0)
            dve.memset(ones_col[:, :], 1.0).then_inc(s_ones, 1)
            dve.memset(scan[:, 1, GE - 1:GE], 0.0)
            dve.memset(acc[:, 0, :], 0.0).then_inc(s_free0, 1)

            dve.wait_ge(s_dst, 48)
            dve.tensor_copy(tmpE[:, :, :], dst_i[:, :].rearrange("p (g j) -> p g j", j=J)).then_inc(s_base, 1)
            dve.wait_ge(s_base, 1)
            dve.wait_ge(s_baseP, 1)
            step(dve.tensor_scalar(baseB[:, :], bank[7][:, 0:NG], float(N - W), 0.0, ALU.min, ALU.max))
            dve.tensor_copy(base_i[:, :], baseB[0:1, :]).then_inc(s_base, 1)
            step(dve.tensor_tensor(rel[:, :, 0, :], tmpE[:, :, :],
                                   baseB[:, :].unsqueeze(2).to_broadcast([P, NG, J]), ALU.subtract))
            dve.wait_ge(s_prv, 48)
            before = prv_i[:, :].rearrange("p (g j) -> p g j", j=J)
            step(dve.tensor_tensor(keep[:, :, :], tmpE[:, :, :], before, ALU.is_equal))
            dve.wait_ge(s_nxt, 48)
            step(dve.tensor_tensor(spare, tmpE[:, :, :], nxt_i[:, :].rearrange("p (g j) -> p g j", j=J),
                                   ALU.not_equal))
            step(dve.scalar_tensor_tensor(out=spare, in0=rel[:, :, 0, :], scalar=1.0, in1=spare,
                                          op0=ALU.add, op1=ALU.mult))
            dve.tensor_scalar_add(rel[:, :, 1, :], spare, -1.0).then_inc(s_rel, 1)
            def one_hot(i, r, cols, s_used, s_made):
                dve.wait_ge(s_used, freed(i, r, R))
                dve.tensor_tensor(S[:, r % R, 0:cols * J, :], iotaW[:, :].unsqueeze(1).to_broadcast([P, cols * J, W]),
                                  rel[:, bass.ds(i * R + r, 1), 0:cols, :].rearrange("p a b j -> p (a b j)")
                                  .unsqueeze(2).to_broadcast([P, cols * J, W]),
                                  ALU.is_equal).then_inc(s_made, 1)

            dve.wait_ge(s_free0, 2)
            dve.wait_ge(s_rel, 1)
            dve.wait_ge(s_iden, 6)
            dve.wait_ge(s_base, 2)
            def turn1(i, steps, live):
                def running_max(r):
                    dve.wait_ge(s_hpT, ready(i, r))
                    dve.wait_ge(s_back, freed(i, r, 2))
                    dve.wait_ge(s_scan, freed(i, r, 1))
                    dve.tensor_tensor_scan(out=scan[:, r % 2, :], data0=keepC[:, r % 2, :],
                                           data1=bank[2 + r % 2][0:D, :],
                                           initial=scan[:, (r + 1) % 2, GE - 1:GE], op0=ALU.mult,
                                           op1=ALU.max).then_inc(s_scan, 1)

                def add_window(r, rows, m, s_part, s_own):
                    base = dve.value_load(base_i[0:1, bass.ds(i * R + r, 1)], min_val=0, max_val=N - W)
                    dve.wait_ge(s_part, ready(i, r))
                    dve.wait_ge(s_own, freed(i, r, 1))
                    a = acc[0:rows, m, bass.ds(base, W)]
                    dve.tensor_tensor(a, a, bank[6 + m][0:rows, 0:W], ALU.add).then_inc(s_own, 1)

                def features(i, r):
                    tiles = own_tiles(i, r)
                    if len(tiles):
                        dve.wait_ge(s_sum, ready(i, r))
                        dve.tensor_copy(xT[0:D, tiles[0] * P:(tiles[-1] + 1) * P], bank[6][0:D, W:W + len(tiles) * P])

                for r in steps:
                    if live(r - 1):
                        features(i, r - 1)
                        add_window(r - 1, DSUM, 0, s_sum, s_acc)
                    if live(r - 4):
                        add_window(r - 4, D, 1, s_max, s_accm)
                    if live(r):
                        one_hot(i, r, 2, s_max, s_S)
                    if live(r - 2):
                        running_max(r - 2)

            def count_descents():
                step(dve.scalar_tensor_tensor(out=spare, in0=before, scalar=0.0, in1=tmpE[:, :, :], op0=ALU.add,
                                              op1=ALU.is_gt, accum_out=bad[:, 0:1]))

            def count_outside():
                step(dve.tensor_scalar(spare, rel[:, :, 0, :], float(W - 1), 0.0, ALU.is_gt, ALU.add,
                                       accum_out=bad[:, 1:2]))
                dve.tensor_tensor(bad[:, 0:1], bad[:, 0:1], bad[:, 1:2], ALU.add).then_inc(s_bad, 1)

            pipeline(dve, turn1, 4, peel=XTURNS + 1, between=(count_descents, count_outside))

            dve.wait_ge(s_acc, NG + AHEAD)
            dve.wait_ge(s_accm, NG + AHEAD)
            dve.wait_ge(s_scan, NG + AHEAD)
            dve.wait_ge(s_flag, 1)
            dve.tensor_copy(flag_i[:, :], bank[7][0:1, 0:1]).then_inc(s_flag_c, 1)
            with irregular(dve):
                with dve.Fori(0, NCH) as c:
                    dve.wait_ge(s_hp, c + 1)
                    dve.tensor_scalar_max(hpT[:, bass.ds(c * CH, CH)], bank[0][0:D, 0:CH], 0.0).then_inc(s_hpc, 1)
                dve.wait_ge(s_hpc, NCH)
                dve.sem_inc(s_used, 1)
                dve.memset(acc[0:DSUM, :, :], 0.0).then_inc(s_edge, 2)
                with dve.Fori(0, NEC) as c:
                    dve.wait_ge(s_ends, c * 32 + 32)
                    dve.sem_inc(s_tick, 1)
                    with dve.Fori(0, EC) as e:
                        a, b = (dve.value_load(ends_i[0:1, n, bass.ds(e, 1)], min_val=0, max_val=N - 1)
                                for n in range(2))
                        dve.wait_ge(s_edge, (c * EC + e) * 2 + 2)
                        dve.sem_inc(s_tick, 1)
                        to_sum, to_max = acc[0:DSUM, 0, bass.ds(b, 1)], acc[0:D, 1, bass.ds(b, 1)]
                        dve.tensor_tensor(to_sum, to_sum, xT[:, bass.ds(a, 1)], ALU.add).then_inc(s_edge, 1)
                        dve.tensor_tensor(to_max, to_max, hpT[:, bass.ds(a, 1)], ALU.max).then_inc(s_edge, 1)
                    dve.sem_inc(s_used, 1)
                dve.wait_ge(s_edge, 2 * E + 2)
                dve.sem_inc(s_made0, 1)

            dve.sem_inc(s_deg, 1)
            dve.wait_ge(s_wb, 128)
            dve.tensor_scalar_mul(w_q[:, :], w_q[:, :], float(HD) ** -0.5)
            dve.wait_ge(s_row, 16)
            step(dve.tensor_scalar_max(counts, counts, 1.0))
            dve.reciprocal(counts, counts).then_inc(s_deg, 1)

            def mean(c):
                a = acc[0:D, 0, bass.ds(c * CH, CH)]
                dve.tensor_tensor(a, a, countsB[:, bass.ds(c * CH, CH)], ALU.mult).then_inc(s_mean, 1)

            def linear(m, first):
                def chunk(i, steps, live):
                    if m == 1 and not live(0):
                        dve.wait_ge(s_row, 48)
                        mean(0)
                        mean(1)
                    for r in steps:
                        if m == 0 and live(r) and live(r - 2):
                            mean(i * 2 + r)
                        if live(r - 2):
                            c = i * 2 + (r - 2)
                            cols = LAST if isinstance(c, int) and c == NCH - 1 else CH
                            dve.wait_ge(s_linc, c + (first + 1))
                            dve.sem_inc(s_tick, 1)
                            dve.bn_stats(stats[:, m, bass.ds(c, 1), :].rearrange("p a c -> p (a c)"),
                                         acc[0:D, m, bass.ds(c * CH, cols)]).then_inc(s_stat, 1)
                return chunk

            pipeline(dve, linear(1, 0), 2, NCH // 2, 2)
            pipeline(dve, linear(0, NCH), 2, NCH // 2, 2)
            dve.wait_ge(s_stat, 2 * NCH)
            for m in range(2):
                step(dve.bn_aggr(mv[:, m, :], stats[:, m, :, :].rearrange("p n c -> p (n c)")))
            dve.sem_inc(s_bn, 1)
            dve.wait_ge(s_std, 1)
            dve.wait_ge(s_gb, 64)
            step(dve.reciprocal(rstd[:, :], std[:, :]))
            gv = gb[:, :].rearrange("p (m k) -> p m k", k=2)
            step(dve.tensor_tensor(ga[:, :], rstd[:, :], gv[:, :, 0], ALU.mult))
            step(dve.tensor_tensor(sh[:, :], ga[:, :], mv[:, :, 0], ALU.mult))
            step(dve.tensor_tensor(sh[:, :], gv[:, :, 1], sh[:, :], ALU.subtract))
            dve.tensor_tensor(shs[:, :], sh[:, 0:1], sh[:, 1:2], ALU.add).then_inc(s_z, 1)

            def layer_norm_stats(i, source, s_st, s_m):
                dve.sem_inc(s_tick, 1)
                for k in range(K7):
                    dve.bn_stats(lnst[:, k, :], source(k)).then_inc(s_st, 1)
                dve.wait_ge(s_st, i * K7 + K7)
                dve.sem_inc(s_tick, 1)
                for k in range(K7):
                    last = dve.bn_aggr(lnmv[:, k, :], lnst[:, k, :])
                last.then_inc(s_m, 1)

            def layer_norm_scale(i, s_s, s_r, s_n):
                dve.wait_ge(s_s, i + 1)
                dve.reciprocal(lnr[:, :], lnr[:, :]).then_inc(s_r, 1)
                dve.wait_ge(s_r, i + 1)
                dve.scalar_tensor_tensor(out=lnb[:, :], in0=lnmv[:, :, 0:1].rearrange("p t a -> p (t a)"),
                                         scalar=-1.0, in1=lnr[:, :], op0=ALU.mult, op1=ALU.mult).then_inc(s_n, 1)

            def nodes(i, steps, live):
                def leaky(t):
                    o1, o2 = acc[0:D, 0, bass.ds(t * KC, KC)], acc[0:D, 1, bass.ds(t * KC, KC)]
                    dve.wait_ge(s_u, t + 1)
                    dve.scalar_tensor_tensor(out=o1, in0=o1, scalar=ga[:, 0:1], in1=o2, op0=ALU.mult,
                                             op1=ALU.add).then_inc(s_z, 1)
                    dve.wait_ge(s_z, t * 2 + 2)
                    dve.scalar_tensor_tensor(out=o2, in0=o1, scalar=0.01, in1=o1, op0=ALU.mult,
                                             op1=ALU.max).then_inc(s_z, 1)

                def copies(t):
                    for n in (0, 2):
                        dve.wait_ge(s_kv, t * 4 + (n + 1))
                        dve.tensor_copy(stage[:, bass.ds(t * K7 + 2 * n, 2), :].rearrange("p a c -> p (a c)"),
                                        bank[KV_BANKS[n]][:, 0:4 * D]).then_inc(s_kvD, 1)

                for r in steps:
                    if live(r - 2):
                        t = i + (r - 2)
                        dve.wait_ge(s_hN, t + 1)
                        layer_norm_stats(t, lambda k: node_rows(t, k), s_lst, s_mv)
                        layer_norm_scale(t, s_sd, s_rs, s_nb)
                    if live(r):
                        leaky(i + r)
                    if live(r - 3):
                        copies(i + (r - 3))

            pipeline(dve, nodes, 3, NK, 1, peel=NK)
            dve.wait_ge(s_free0, 3)

            def general_attention(dve):
                dve.wait_ge(s_kvtab, 16 * (NK + 1))
                with dve.Fori(0, NCH) as c:
                    at = bass.ds(c * CH, CH)
                    dve.wait_ge(s_kqv, c + 1)
                    for n, to in enumerate((kT, qT, vT)):
                        last = dve.tensor_copy(to[:, at], bank[n][0:D, 0:CH])
                    last.then_inc(s_kqvc, 1)
                dve.wait_ge(s_kqvc, NCH)
                dve.memset(msgs[D:DMSG, 0:EC], 1.0)
                dve.sem_inc(s_used2, 1)
                dve.memset(acc[0:DMSG, 0, :], 0.0).then_inc(s_edge2, 1)
                dve.wait_ge(s_edge2, 1)
                with dve.Fori(0, NEC) as c:
                    dve.wait_ge(s_ends2, c * 48 + 48)
                    dve.sem_inc(s_tick, 1)
                    with dve.Fori(0, EC) as e:
                        a, b = (dve.value_load(ends_i[0:1, n, bass.ds(e, 1)], min_val=0, max_val=N - 1)
                                for n in range(2))
                        dve.tensor_tensor(kq[:, bass.ds(e, 1)], kT[:, bass.ds(a, 1)], qT[:, bass.ds(b, 1)],
                                          ALU.mult).then_inc(s_kq, 1)
                        dve.tensor_copy(vE[0:D, bass.ds(e, 1)], vT[:, bass.ds(a, 1)]).then_inc(s_kq, 1)
                    dve.wait_ge(s_kq, (c + 1) * (2 * EC))
                    dve.wait_ge(s_eE, c + 1)
                    dve.tensor_tensor(kq, kq, bank[1][0:D, 0:EC], ALU.mult).then_inc(s_kqe, 1)
                    dve.wait_ge(s_dot, c + 1)
                    dve.tensor_scalar(weight, bank[2][0:DMSG, 0:EC], 5.0, -5.0, ALU.min, ALU.max
                                      ).then_inc(s_dotc, 1)
                    dve.wait_ge(s_w2, c + 1)
                    dve.tensor_tensor(weighted, vE, weight, ALU.mult).then_inc(s_wd, 1)
                    dve.wait_ge(s_wd, c + 1)
                    dve.sem_inc(s_tick, 1)
                    with dve.Fori(0, EC) as e:
                        b = dve.value_load(ends_i[0:1, 1, bass.ds(e, 1)], min_val=0, max_val=N - 1)
                        dve.wait_ge(s_edge2, c * EC + e + 1)
                        dve.sem_inc(s_tick, 1)
                        to = acc[0:DMSG, 0, bass.ds(b, 1)]
                        dve.tensor_tensor(to, to, weighted[:, bass.ds(e, 1)], ALU.add).then_inc(s_edge2, 1)
                    dve.sem_inc(s_used2, 1)
                dve.wait_ge(s_edge2, E + 1)
                dve.sem_inc(s_made1, 1)

            def turn2(i, steps, live):
                def products_e(r):
                    b = r % 2
                    dve.wait_ge(s_kvg[r % R], landed(i, r, 16 * J))
                    dve.wait_ge(s_EQ, ready(i, r))
                    dve.wait_ge(s_p3, freed(i, r, 2))
                    dve.tensor_tensor(prod[:, b, :].rearrange("p (j c) -> p j c", j=J), kvg[:, r % R, :, 0:D],
                                      bank[2 + b][:, 0:J * D].rearrange("p (j c) -> p j c", j=J),
                                      ALU.mult).then_inc(s_p1, 1)

                def products_q(r):
                    b = r % 2
                    dve.wait_ge(s_p1, ready(i, r))
                    dve.tensor_tensor(prod[:, b, :], prod[:, b, :], bank[4 + b][:, 0:J * D],
                                      ALU.mult).then_inc(s_p2, 1)

                def head_sums(r):
                    b = r % 2
                    dve.wait_ge(s_p2, ready(i, r))
                    dve.wait_ge(s_exp, freed(i, r, 2))
                    dve.reduce_sum(sc[:, b, :], prod[:, b, :].rearrange("p (h d) -> p h d", d=HD),
                                   AX.X).then_inc(s_p3, 1)

                def queries(r):
                    dve.wait_ge(s_q, ready(i, r))
                    dve.wait_ge(s_agg, freed(i, r, 3))
                    dve.wait_ge(s_EQ, freed(i, r, 2))
                    dve.tensor_copy(qwin[:, r % 2, :], bank[6 + (r + 1) % 2][0:W, W:W + D]).then_inc(s_qc, 1)

                def clip(r):
                    b = r % 2
                    dve.wait_ge(s_p3, ready(i, r))
                    dve.tensor_scalar(sc[:, b, :], sc[:, b, :], 5.0, -5.0, ALU.min, ALU.max).then_inc(s_clip, 1)

                def message(r):
                    b = r % 2
                    dve.wait_ge(s_exp, ready(i, r))
                    dve.tensor_tensor(msg[:, b, :, 0:D].rearrange("p j (h d) -> p j h d", d=HD),
                                      kvg[:, r % R, :, D:2 * D].rearrange("p j (h d) -> p j h d", d=HD),
                                      msg[:, b, :, D:DMSG].unsqueeze(3).to_broadcast([P, J, H, HD]),
                                      ALU.mult).then_inc(s_msg, 1)

                def add_window(r):
                    base = dve.value_load(base_i[0:1, bass.ds(i * R + r, 1)], min_val=0, max_val=N - W)
                    dve.wait_ge(s_agg, ready(i, r))
                    dve.wait_ge(s_acc2, freed(i, r, 1))
                    a = acc[0:DMSG, 0, bass.ds(base, W)]
                    dve.tensor_tensor(a, a, bank[6 + r % 2][0:DMSG, 0:W], ALU.add).then_inc(s_acc2, 1)

                for r in steps:
                    if live(r):
                        one_hot(i, r, 1, s_agg, s_S2)
                    if live(r - 2):
                        products_e(r - 2)
                    if live(r - 2):
                        products_q(r - 2)
                    if live(r - 3):
                        message(r - 3)
                    if live(r - 2):
                        head_sums(r - 2)
                    if live(r - 4):
                        add_window(r - 4)
                    if live(r - 2):
                        clip(r - 2)
                    if live(r):
                        queries(r)

            pipeline(dve, turn2, 4)

            with irregular(dve):
                general_attention(dve)

            def last_norm(i, steps, live):
                parts = []
                for h, (k0, k1) in enumerate(HALVES):
                    rows = bank[i % 2 * 2 + h][:, 0:(k1 - k0) * DMSG]
                    parts.append((k0, k1, rows.rearrange("p (k c) -> p k c", c=DMSG)))
                if live(0):
                    dve.wait_ge(s_wv, i + 1)
                    wait_past(dve, s_hn, i * 2)
                    for k0, k1, rows in parts:
                        last = dve.tensor_scalar_add(nz[:, k0:k1, :], rows[:, :, D:DMSG], 1e-6)
                    last.then_inc(s_nz, 1)
                    dve.wait_ge(s_nz, i * 2 + 1)
                    dve.reciprocal(nz[:, :, :], nz[:, :, :]).then_inc(s_nz, 1)
                if live(-1):
                    t = i - 1
                    dve.wait_ge(s_add, t * 2 + 2)
                    wait_past(dve, s_mv2, t)
                    layer_norm_stats(t, lambda k: xN[:, t * K7 + k, :], s_lst2, s_mv2)
                if live(0):
                    dve.wait_ge(s_nz, i * 2 + 2)
                    wait_past(dve, s_add, i * 2)
                    for k0, k1, rows in parts:
                        dve.tensor_tensor(hn[:, k0:k1, :].rearrange("p k (h d) -> p k h d", d=HD),
                                          rows[:, :, 0:D].rearrange("p k (h d) -> p k h d", d=HD),
                                          nz[:, k0:k1, :].unsqueeze(3).to_broadcast([P, k1 - k0, H, HD]),
                                          ALU.mult).then_inc(s_hn, 1)
                    k0, k1 = HALVES[0]
                    own = xN[:, i * K7:i * K7 + k1, :]
                    dve.wait_ge(s_hn, i * 2 + 1)
                    dve.tensor_tensor(own, own, hn[:, k0:k1, :], ALU.add).then_inc(s_add, 1)
                if live(-1):
                    layer_norm_scale(i - 1, s_sd2, s_rs2, s_nb2)

            pipeline(dve, last_norm, 1, NK, 1, peel=NK)

        @block.tensor
        def _(pe):
            for s in (s_xe, s_hpT, s_sum, s_back, s_max, s_Te, s_T, s_q, s_EQ, s_agg):
                pe.sem_inc(s, AHEAD)
            pe.wait_ge(s_iden, 6)
            pe.wait_ge(s_base, 1)
            pe.matmul(bank[7][:, 0:NG], first_row[:, :], tmpE[:, :, 0], start=True, stop=True).then_inc(s_baseP, 1)
            pe.wait_ge(s_wp, 32)
            pe.wait_ge(s_rel, 1)

            def turn1(i, steps, live):
                def front(r):
                    pe.wait_ge(s_gat[r], landed(i, r, 16 * J))
                    pe.wait_ge(s_xec, freed(i, r, 1))
                    for j in range(J):
                        pe.transpose(bank[0][0:D, j:GE:J], xg[:, r, j, 0:D], ident[:, :])
                    for j in range(J):
                        last = pe.matmul(bank[1][0:D, j:GE:J],
                                         keep[:, bass.ds(i * R + r, 1), j].to_broadcast([P, D]), identb[:, :],
                                         start=True, stop=True)
                    last.then_inc(s_xe, 1)

                def pool_layer(r):
                    b = r % 2
                    pe.wait_ge(s_xec, ready(i, r))
                    pe.wait_ge(s_scan, freed(i, r, 2))
                    pe.matmul(bank[2 + b][0:D, :], w_pool[:, :], xeC[:, b, :], start=True,
                              stop=True).then_inc(s_hpT, 1)

                def sums(r):
                    pe.wait_ge(s_S, ready(i, r))
                    pe.wait_ge(s_acc, freed(i, r, 1))
                    for n, t in enumerate(own_tiles(i, r)):
                        pe.wait_ge(s_x[t // K7], 32 if t // K7 == NK - 1 else 16)
                        pe.transpose(bank[6][0:D, W + n * P:W + (n + 1) * P], xN[:, t, :], ident[:, :])
                    for j in range(J):
                        last = pe.matmul(bank[6][0:DSUM, 0:W], xg[:, r, j, :], S[:, r % R, j, :],
                                         start=j == 0, stop=j == J - 1)
                    last.then_inc(s_sum, 1)

                def back(r):
                    b = r % 2
                    pe.wait_ge(s_scan, ready(i, r))
                    pe.wait_ge(s_bcp, freed(i, r, 2))
                    for j in range(J):
                        last = pe.transpose(bank[4 + b][:, j * D:(j + 1) * D], scan[:, b, j:GE:J], ident[0:D, 0:D])
                    last.then_inc(s_back, 1)

                def ends(r):
                    b = r % 2
                    pe.wait_ge(s_bcp, ready(i, r))
                    pe.wait_ge(s_accm, freed(i, r, 1))
                    for j in range(J):
                        last = pe.matmul(bank[7][0:D, 0:W], scanE[:, b, j, :], S[:, r % R, J + j, :],
                                         start=j == 0, stop=j == J - 1)
                    last.then_inc(s_max, 1)

                for r in steps:
                    if live(r):
                        front(r)
                    if live(r - 1):
                        pool_layer(r - 1)
                    if live(r - 3):
                        ends(r - 3)
                    if live(r):
                        sums(r)
                    if live(r - 2):
                        back(r - 2)

            pipeline(pe, turn1, 3, peel=XTURNS)

            pe.wait_ge(s_acc, NG + AHEAD)
            pe.wait_ge(s_accm, NG + AHEAD)
            pe.wait_ge(s_bad, 1)
            pe.matmul(bank[7][0:1, 0:1], bad[:, 0:1], ones_col[:, :], start=True, stop=True).then_inc(s_flag, 1)
            with irregular(pe):
                with pe.Fori(0, NCH) as c:
                    pe.matmul(bank[0][0:D, 0:CH], w_pool[:, :], xT[:, bass.ds(c * CH, CH)], start=True,
                              stop=True).then_inc(s_hp, 1)
                    pe.wait_ge(s_hpc, c + 1)
                pe.wait_ge(s_made0, 1)
            pe.wait_ge(s_w, 64)

            def linear(m, first, ws, wn):
                def chunk(i, steps, live):
                    for r in steps:
                        c = i * 2 + r
                        at = bass.ds(c * CH, CH)
                        if m == 0:
                            pe.wait_ge(s_mean, c + 1)
                        wait_past(pe, s_linc, c + (first - 1))
                        o = bank[r % 2][0:D, 0:CH]
                        pe.matmul(o, ws[:, :], xT[0:D, at], start=True, stop=False)
                        pe.matmul(o, wn[:, :], acc[0:D, m, at], start=False, stop=True).then_inc(s_lin, 1)
                return chunk

            pipeline(pe, linear(1, 0, w_self2, w_neigh2), 0, NCH // 2, 2, peel=1)
            pipeline(pe, linear(0, NCH, w_self1, w_neigh1), 0, NCH // 2, 2)

            def stay_warm(times, b):
                for _ in range(times):
                    pe.matmul(bank[b][:, 0:CH], ident[0:D, :], xT[0:D, 0:CH], start=True, stop=True)

            stay_warm(9, 7)

            for i in range(NK + 3):
                t = i - 3
                if t >= 0:
                    pe.wait_ge(s_x1, t + 1)
                    wait_past(pe, s_kvD, 2 * t)
                    wait_past(pe, s_kvA, 2 * t)
                    for k in range(K7):
                        last = pe.transpose(bank[4 + k // 4][0:D, (k % 4) * P:(k % 4 + 1) * P],
                                            xN[:, t * K7 + k, :], ident[:, :])
                    last.then_inc(s_x1T, 1)
                if 1 <= i <= NK:
                    pe.wait_ge(s_h, i)
                    wait_past(pe, s_x1, i - 2)
                    for k in range(K7):
                        at = ((i - 1) * K7 + k) * P
                        last = pe.transpose(node_rows(i - 1, k), acc[0:D, 0, at:at + P], ident[0:D, 0:D])
                    last.then_inc(s_hN, 1)
                if i == 2:
                    stay_warm(4, 7)
                if t >= 0:
                    pe.wait_ge(s_x1c, t + 1)
                    for n in range(4):
                        for k in range(2 * n, min(2 * n + 2, K7)):
                            last = pe.matmul(bank[KV_BANKS[n]][:, (k % 2) * 2 * D:(k % 2 + 1) * 2 * D],
                                             xT[:, (t * K7 + k) * P:(t * K7 + k + 1) * P], w_kv[:, :],
                                             start=True, stop=True)
                        last.then_inc(s_kv, 1)

            pe.wait_ge(s_kvA, 2 * NK)
            pe.wait_ge(s_kvD, 2 * NK)

            def turn2(i, steps, live):
                def transposes(r):
                    b = r % 2
                    pe.wait_ge(s_ea[r], i * 16 + 16)
                    pe.wait_ge(s_ec, freed(i, r, 1))
                    for j in range(J):
                        last = pe.transpose(bank[0][0:D, j * P:(j + 1) * P], ea[:, r, j, :], ident[:, :])
                    last.then_inc(s_Te, 1)
                    pe.wait_ge(s_tc, freed(i, r, 1))
                    pe.sem_inc(s_tick, 1)
                    pe.wait_ge(s_S2, ready(i, r))
                    pe.sem_inc(s_tick, 1)
                    for j in range(J):
                        last = pe.transpose(bank[1][0:W, j * P:(j + 1) * P], S[:, r % R, j, :], ident[:, :])
                    last.then_inc(s_T, 1)

                def expand(r):
                    b = r % 2
                    pe.wait_ge(s_ec, ready(i, r))
                    pe.wait_ge(s_p2, freed(i, r, 2))
                    for j in range(J):
                        pe.matmul(bank[2 + b][:, j * D:(j + 1) * D], eaC[:, b, j * P:(j + 1) * P], w_e[:, :],
                                  start=True, stop=True)
                    pe.wait_ge(s_tc, ready(i, r))
                    pe.wait_ge(s_qc, ready(i, r))
                    for j in range(J):
                        last = pe.matmul(bank[4 + b][:, j * D:(j + 1) * D], stC[:, b, j * P:(j + 1) * P],
                                         qwin[:, b, :], start=True, stop=True)
                    last.then_inc(s_EQ, 1)

                def queries(r):
                    pe.wait_ge(s_xw, ready(i, r))
                    wait_past(pe, s_acc2, freed(i, r, 5))
                    pe.wait_ge(s_qc, freed(i, r, 2))
                    pe.matmul(bank[6 + (r + 1) % 2][0:W, W:W + D], xwin[:, r % 2, :], w_q[:, :], start=True,
                              stop=True).then_inc(s_q, 1)

                def aggregate(r):
                    b = r % 2
                    pe.wait_ge(s_msg, ready(i, r))
                    pe.wait_ge(s_acc2, freed(i, r, 2))
                    for j in range(J):
                        last = pe.matmul(bank[6 + b][0:DMSG, 0:W], msg[:, b, j, :], S[:, r % R, j, :],
                                         start=j == 0, stop=j == J - 1)
                    last.then_inc(s_agg, 1)

                for r in steps:
                    if live(r - 1):
                        expand(r - 1)
                    if live(r):
                        transposes(r)
                        queries(r)
                    if isinstance(i, int) and i == 0 and r == 2:
                        pe.wait_ge(s_qc, ready(0, 1))
                        stay_warm(3, 6)
                    if live(r - 3):
                        aggregate(r - 3)

            pipeline(pe, turn2, 3)

            pe.wait_ge(s_acc2, NG + AHEAD)
            with irregular(pe):
                with pe.Fori(0, NCH) as c:
                    at = bass.ds(c * CH, CH)
                    for n, w in enumerate((w_kv[:, 0:D], w_q[:, :], w_kv[:, D:2 * D])):
                        last = pe.matmul(bank[n][0:D, 0:CH], w, xT[:, at], start=True, stop=True)
                    last.then_inc(s_kqv, 1)
                    pe.wait_ge(s_kqvc, c + 1)
                pe.wait_ge(s_mask, 5)
                with pe.Fori(0, NEC) as c:
                    pe.wait_ge(s_ends2, c * 48 + 48)
                    pe.transpose(bank[0][0:D, 0:EC], ea[0:EC, 0, 0, :], ident[0:EC, 0:EC]).then_inc(s_eaT, 1)
                    pe.wait_ge(s_eaTc, c + 1)
                    pe.matmul(bank[1][0:D, 0:EC], w_e[:, :], eaC[:, 0, 0:EC], start=True, stop=True).then_inc(s_eE, 1)
                    pe.wait_ge(s_kqe, c + 1)
                    pe.matmul(bank[2][0:DMSG, 0:EC], same_head, kq, start=True, stop=True).then_inc(s_dot, 1)
                    pe.wait_ge(s_dotc, c + 1)
                pe.wait_ge(s_made1, 1)

            for i in range(NK):
                wait_past(pe, s_hn, (i - 1) * 2)
                for k in range(K7):
                    at = (i * K7 + k) * P
                    last = pe.transpose(bank[i % 2 * 2 + k // 4][:, (k % 4) * DMSG:(k % 4 + 1) * DMSG], acc[0:DMSG, 0, at:at + P],
                                        ident[0:DMSG, 0:DMSG])
                last.then_inc(s_wv, 1)


_WEIGHTS = ['L0_gnn_W_self1', 'L0_gnn_W_neigh1', 'L0_gnn_W_pool', 'L0_gnn_b_pool', 'L0_gnn_W_self2', 'L0_gnn_W_neigh2',
            'L0_gnn_g1', 'L0_gnn_beta1', 'L0_gnn_g2', 'L0_gnn_beta2', 'L1_gnn_Wq', 'L1_gnn_bq', 'L1_gnn_Wk',
            'L1_gnn_bk', 'L1_gnn_We', 'L1_gnn_be', 'L1_gnn_Wv', 'L1_gnn_bv']


def kernel(**inputs):
    import numpy as _np
    import concourse.bacc as _bacc
    from concourse import mybir as _mybir
    from concourse.bass_utils import run_bass_kernel_spmd as _run

    def split(a):
        whole = a[:FULL * GE].reshape(FULL, P, J).transpose(1, 0, 2).reshape(P, FULL * J)
        return _np.ascontiguousarray(whole), _np.ascontiguousarray(a[FULL * GE:])

    src, dst = _np.asarray(inputs['src']), _np.asarray(inputs['dst'])
    named = [('x', inputs['x']), ('src', src), ('dst', dst)]
    for name, a in (('src', src), ('dst', dst), ('before', _np.concatenate([dst[:1], dst[:-1]])), ('after', dst[1:])):
        whole, rest = split(a)
        named += [(name + '_groups', whole), (name + '_rest', rest)]
    named += [('edge_attr', inputs['edge_attr_96'])] + [(n, inputs[n]) for n in _WEIGHTS]
    nc = _bacc.Bacc("TRN2", target_bir_lowering=False, num_devices=1)
    arrays, args = {}, []
    for name, a in named:
        a = _np.ascontiguousarray(a)
        arrays[f"in_{name}_dram"] = a
        args.append(nc.dram_tensor(f"in_{name}_dram", a.shape, _mybir.dt.from_np(a.dtype), kind="ExternalInput").ap())
    args.append(nc.dram_tensor("out_0_dram", (N, D), _mybir.dt.float32, kind="ExternalOutput").ap())
    build(nc, *args)
    return _run(nc, [arrays], core_ids=[0]).results[0]["out_0_dram"]
```
